# Optimizing a Trainium2 kernel written in Bass

```python
import numpy as np
import jax
import jax.numpy as jnp

def _softmax(x, axis=-1):
    return jax.nn.softmax(x, axis=axis)

def _gelu(x):
    return jax.nn.gelu(x, approximate=True)

def _silu(x):
    return jax.nn.silu(x)

def _sigmoid(x):
    return jax.nn.sigmoid(x)

def _layernorm(x, axis=-1, eps=1e-05):
    m = jnp.mean(x, axis=axis, keepdims=True)
    v = jnp.var(x, axis=axis, keepdims=True)
    return (x - m) / jnp.sqrt(v + eps)

def _scatter_add(tgt, idx, src, axis=0):
    return tgt.at[idx].add(src)

def _segment_sum(src, seg, n):
    return jax.ops.segment_sum(src, seg, n)
kernel_name = 'mk_prb_d1_jaxref_r8_f93c16'

def setup_inputs(seed: int=0):
    np.random.seed(seed)
    _w = jnp.asarray

    def _L0_attn_setup():
        import jax, jax.numpy as jnp
        import numpy as np
        import math
        B, L, HID = (2, 512, 128)
        NH, DK, DV = (12, 64, 128)
        KD, VD, CS = (NH * DK, NH * DV, 4)
        SCALE = DK ** (-0.5)

        def _causal_depthwise_conv(x, w):
            c, k = w.shape
            xt = jnp.transpose(x, (0, 2, 1))
            out = jax.lax.conv_general_dilated(xt, w[:, None, :], window_strides=(1,), padding=[(k - 1, 0)], feature_group_count=c, dimension_numbers=('NCH', 'OIH', 'NCH'))
            return jnp.transpose(out, (0, 2, 1))

        def _l2norm(x, eps=1e-06):
            return x * jax.lax.rsqrt(jnp.sum(x * x, axis=-1, keepdims=True) + eps)

        def _gated_delta_net(hidden_states, Wq, Wk, Wv, Wg, Wo, conv_q, conv_k, conv_v, Wgk, Wb, b_b, A_log, dt_bias, g_norm_weight):
            b, l, _ = hidden_states.shape
            q = jax.nn.silu(_causal_depthwise_conv(hidden_states @ Wq, conv_q))
            k = jax.nn.silu(_causal_depthwise_conv(hidden_states @ Wk, conv_k))
            v = jax.nn.silu(_causal_depthwise_conv(hidden_states @ Wv, conv_v))
            gk = -jnp.exp(A_log) * jax.nn.softplus(hidden_states @ Wgk + dt_bias)
            beta = jax.nn.sigmoid(hidden_states @ Wb + b_b)
            q = jnp.transpose(q.reshape(b, l, NH, DK), (0, 2, 1, 3))
            k = jnp.transpose(k.reshape(b, l, NH, DK), (0, 2, 1, 3))
            v = jnp.transpose(v.reshape(b, l, NH, DV), (0, 2, 1, 3))
            q = _l2norm(q) * SCALE
            k = _l2norm(k)
            qs = jnp.moveaxis(q, 2, 0)
            ks_ = jnp.moveaxis(k, 2, 0)
            vs = jnp.moveaxis(v, 2, 0)
            bs = jnp.moveaxis(beta, 1, 0)
            gs = jnp.moveaxis(gk, 1, 0)

            def step(S, inp):
                qt, kt, vt, bt, gt = inp
                S = S * jnp.exp(gt)[..., None, None]
                kv = jnp.einsum('bhk,bhkv->bhv', kt, S)
                delta = (vt - kv) * bt[..., None]
                S = S + jnp.einsum('bhk,bhv->bhkv', kt, delta)
                ot = jnp.einsum('bhk,bhkv->bhv', qt, S)
                return (S, ot)
            S0 = jnp.zeros((b, NH, DK, DV), hidden_states.dtype)
            _, os_ = jax.lax.scan(step, S0, (qs, ks_, vs, bs, gs))
            o = jnp.moveaxis(os_, 0, 1)
            g = (hidden_states @ Wg).reshape(b, l, NH, DV)
            var = jnp.mean(o * o, axis=-1, keepdims=True)
            o = o * jax.lax.rsqrt(var + 1e-05) * g_norm_weight
            o = o * g * jax.nn.sigmoid(g)
            return o.reshape(b, l, VD) @ Wo
        key = jax.random.key(seed)
        ks = jax.random.split(key, 16)
        rn = lambda i, shape, s: jax.random.normal(ks[i], shape, jnp.float32) * s
        hidden_states = rn(0, (B, L, HID), 1.0)
        Wq = rn(1, (HID, KD), HID ** (-0.5))
        Wk = rn(2, (HID, KD), HID ** (-0.5))
        Wv = rn(3, (HID, VD), HID ** (-0.5))
        Wg = rn(4, (HID, VD), HID ** (-0.5))
        Wo = rn(5, (VD, HID), VD ** (-0.5))
        conv_q = rn(6, (KD, CS), 0.5)
        conv_k = rn(7, (KD, CS), 0.5)
        conv_v = rn(8, (VD, CS), 0.5)
        Wgk = rn(9, (HID, NH), HID ** (-0.5))
        Wb = rn(10, (HID, NH), HID ** (-0.5))
        b_b = rn(11, (NH,), 0.1)
        A = jax.random.uniform(ks[12], (NH,), jnp.float32, 0.5, 16.0)
        A_log = jnp.log(A)
        dt = jnp.exp(jax.random.uniform(ks[13], (NH,), jnp.float32) * (math.log(0.1) - math.log(0.001)) + math.log(0.001))
        dt = jnp.clip(dt, 0.0001, None)
        dt_bias = dt + jnp.log(-jnp.expm1(-dt))
        g_norm_weight = jnp.ones((DV,), jnp.float32)
        return dict(hidden_states=hidden_states, Wq=Wq, Wk=Wk, Wv=Wv, Wg=Wg, Wo=Wo, conv_q=conv_q, conv_k=conv_k, conv_v=conv_v, Wgk=Wgk, Wb=Wb, b_b=b_b, A_log=A_log, dt_bias=dt_bias, g_norm_weight=g_norm_weight)
    _L0_attn_in = _L0_attn_setup()

    def _L0_ffn_setup():
        import jax, jax.numpy as jnp
        import numpy as np
        BLOCK = 16
        _GRID = jnp.array([0.0, 0.5, 1.0, 1.5, 2.0, 3.0, 4.0, 6.0], dtype=jnp.float32)
        _MID = jnp.array([0.25, 0.75, 1.25, 1.75, 2.5, 3.5, 5.0], dtype=jnp.float32)

        def fp4_quant_dequant(x):
            shape = x.shape
            xb = x.reshape(shape[:-1] + (shape[-1] // BLOCK, BLOCK))
            scale = jnp.max(jnp.abs(xb), axis=-1, keepdims=True) / 6.0
            scale = jnp.maximum(scale, jnp.float32(1e-12))
            xn = xb / scale
            idx = jnp.searchsorted(_MID, jnp.abs(xn))
            q = _GRID[idx] * jnp.sign(xn) * scale
            return q.reshape(shape)

        def fp4_linear(x, w):
            xq = fp4_quant_dequant(x)
            wq = fp4_quant_dequant(w)
            return jnp.einsum('bsk,nk->bsn', xq, wq)
        key = jax.random.key(seed)
        k1, k2, k3, k4 = jax.random.split(key, 4)
        H, I = (128, 352)
        x = jax.random.normal(k1, (4, 512, H), dtype=jnp.float32)
        w_gate = jax.random.normal(k2, (I, H), dtype=jnp.float32) * 0.02
        w_up = jax.random.normal(k3, (I, H), dtype=jnp.float32) * 0.02
        w_down = jax.random.normal(k4, (H, I), dtype=jnp.float32) * 0.02
        return {'x': x, 'w_gate': w_gate, 'w_up': w_up, 'w_down': w_down}
    _L0_ffn_in = _L0_ffn_setup()
    _d = {'L0_attn_hidden_states': _L0_attn_in['hidden_states'], 'L0_attn_Wq': _L0_attn_in['Wq'], 'L0_attn_Wk': _L0_attn_in['Wk'], 'L0_attn_Wv': _L0_attn_in['Wv'], 'L0_attn_Wg': _L0_attn_in['Wg'], 'L0_attn_Wo': _L0_attn_in['Wo'], 'L0_attn_conv_q': _L0_attn_in['conv_q'], 'L0_attn_conv_k': _L0_attn_in['conv_k'], 'L0_attn_conv_v': _L0_attn_in['conv_v'], 'L0_attn_Wgk': _L0_attn_in['Wgk'], 'L0_attn_Wb': _L0_attn_in['Wb'], 'L0_attn_b_b': _L0_attn_in['b_b'], 'L0_attn_A_log': _L0_attn_in['A_log'], 'L0_attn_dt_bias': _L0_attn_in['dt_bias'], 'L0_attn_g_norm_weight': _L0_attn_in['g_norm_weight'], 'L0_ffn_w_gate': _L0_ffn_in['w_gate'], 'L0_ffn_w_up': _L0_ffn_in['w_up'], 'L0_ffn_w_down': _L0_ffn_in['w_down']}
    _x0 = _d['L0_attn_hidden_states']
    _d['L0_attn_hidden_states'] = jax.random.normal(jax.random.fold_in(jax.random.key(seed), 1), (32, 256, 128), dtype=_x0.dtype)
    del _x0
    return _d

def reference(L0_attn_hidden_states, L0_attn_Wq, L0_attn_Wk, L0_attn_Wv, L0_attn_Wg, L0_attn_Wo, L0_attn_conv_q, L0_attn_conv_k, L0_attn_conv_v, L0_attn_Wgk, L0_attn_Wb, L0_attn_b_b, L0_attn_A_log, L0_attn_dt_bias, L0_attn_g_norm_weight, L0_ffn_w_gate, L0_ffn_w_up, L0_ffn_w_down):

    def _L0_attn_ref(hidden_states, Wq, Wk, Wv, Wg, Wo, conv_q, conv_k, conv_v, Wgk, Wb, b_b, A_log, dt_bias, g_norm_weight):
        import jax, jax.numpy as jnp
        import numpy as np
        import math
        B, L, HID = (2, 512, 128)
        NH, DK, DV = (12, 64, 128)
        KD, VD, CS = (NH * DK, NH * DV, 4)
        SCALE = DK ** (-0.5)

        def _causal_depthwise_conv(x, w):
            c, k = w.shape
            xt = jnp.transpose(x, (0, 2, 1))
            out = jax.lax.conv_general_dilated(xt, w[:, None, :], window_strides=(1,), padding=[(k - 1, 0)], feature_group_count=c, dimension_numbers=('NCH', 'OIH', 'NCH'))
            return jnp.transpose(out, (0, 2, 1))

        def _l2norm(x, eps=1e-06):
            return x * jax.lax.rsqrt(jnp.sum(x * x, axis=-1, keepdims=True) + eps)

        def _gated_delta_net(hidden_states, Wq, Wk, Wv, Wg, Wo, conv_q, conv_k, conv_v, Wgk, Wb, b_b, A_log, dt_bias, g_norm_weight):
            b, l, _ = hidden_states.shape
            q = jax.nn.silu(_causal_depthwise_conv(hidden_states @ Wq, conv_q))
            k = jax.nn.silu(_causal_depthwise_conv(hidden_states @ Wk, conv_k))
            v = jax.nn.silu(_causal_depthwise_conv(hidden_states @ Wv, conv_v))
            gk = -jnp.exp(A_log) * jax.nn.softplus(hidden_states @ Wgk + dt_bias)
            beta = jax.nn.sigmoid(hidden_states @ Wb + b_b)
            q = jnp.transpose(q.reshape(b, l, NH, DK), (0, 2, 1, 3))
            k = jnp.transpose(k.reshape(b, l, NH, DK), (0, 2, 1, 3))
            v = jnp.transpose(v.reshape(b, l, NH, DV), (0, 2, 1, 3))
            q = _l2norm(q) * SCALE
            k = _l2norm(k)
            qs = jnp.moveaxis(q, 2, 0)
            ks_ = jnp.moveaxis(k, 2, 0)
            vs = jnp.moveaxis(v, 2, 0)
            bs = jnp.moveaxis(beta, 1, 0)
            gs = jnp.moveaxis(gk, 1, 0)

            def step(S, inp):
                qt, kt, vt, bt, gt = inp
                S = S * jnp.exp(gt)[..., None, None]
                kv = jnp.einsum('bhk,bhkv->bhv', kt, S)
                delta = (vt - kv) * bt[..., None]
                S = S + jnp.einsum('bhk,bhv->bhkv', kt, delta)
                ot = jnp.einsum('bhk,bhkv->bhv', qt, S)
                return (S, ot)
            S0 = jnp.zeros((b, NH, DK, DV), hidden_states.dtype)
            _, os_ = jax.lax.scan(step, S0, (qs, ks_, vs, bs, gs))
            o = jnp.moveaxis(os_, 0, 1)
            g = (hidden_states @ Wg).reshape(b, l, NH, DV)
            var = jnp.mean(o * o, axis=-1, keepdims=True)
            o = o * jax.lax.rsqrt(var + 1e-05) * g_norm_weight
            o = o * g * jax.nn.sigmoid(g)
            return o.reshape(b, l, VD) @ Wo
        return _gated_delta_net(hidden_states, Wq, Wk, Wv, Wg, Wo, conv_q, conv_k, conv_v, Wgk, Wb, b_b, A_log, dt_bias, g_norm_weight)

    def _L0_ffn_ref(x, w_gate, w_up, w_down):
        import jax, jax.numpy as jnp
        import numpy as np
        BLOCK = 16
        _GRID = jnp.array([0.0, 0.5, 1.0, 1.5, 2.0, 3.0, 4.0, 6.0], dtype=jnp.float32)
        _MID = jnp.array([0.25, 0.75, 1.25, 1.75, 2.5, 3.5, 5.0], dtype=jnp.float32)

        def fp4_quant_dequant(x):
            shape = x.shape
            xb = x.reshape(shape[:-1] + (shape[-1] // BLOCK, BLOCK))
            scale = jnp.max(jnp.abs(xb), axis=-1, keepdims=True) / 6.0
            scale = jnp.maximum(scale, jnp.float32(1e-12))
            xn = xb / scale
            idx = jnp.searchsorted(_MID, jnp.abs(xn))
            q = _GRID[idx] * jnp.sign(xn) * scale
            return q.reshape(shape)

        def fp4_linear(x, w):
            xq = fp4_quant_dequant(x)
            wq = fp4_quant_dequant(w)
            return jnp.einsum('bsk,nk->bsn', xq, wq)
        gate = fp4_linear(x, w_gate)
        y = fp4_linear(x, w_up)
        h = jax.nn.silu(gate) * y
        return fp4_linear(h, w_down)
    x = L0_attn_hidden_states
    xn = _layernorm(x, axis=-1)
    x = x + _L0_attn_ref(xn, L0_attn_Wq, L0_attn_Wk, L0_attn_Wv, L0_attn_Wg, L0_attn_Wo, L0_attn_conv_q, L0_attn_conv_k, L0_attn_conv_v, L0_attn_Wgk, L0_attn_Wb, L0_attn_b_b, L0_attn_A_log, L0_attn_dt_bias, L0_attn_g_norm_weight) + _L0_ffn_ref(xn, L0_ffn_w_gate, L0_ffn_w_up, L0_ffn_w_down)
    return x

_drawn_inputs = setup_inputs


def setup_inputs(seed=0):
    import zlib

    import numpy as np

    out = dict(_drawn_inputs(seed))
    spreads = {'L0_attn_g_norm_weight': (1.0, 0.2)}
    factors = {'L0_attn_b_b': 32.589,
     'L0_ffn_w_gate': 6.568,
     'L0_ffn_w_up': 6.448,
     'L0_ffn_w_down': 6.477}
    for name, (base, spread) in spreads.items():
        noise = np.random.default_rng([zlib.crc32(name.encode()), seed]).standard_normal(out[name].shape)
        drawn = base * np.exp(spread * noise) if base else spread * noise
        out[name] = jnp.asarray(drawn.astype(out[name].dtype))
    for name, factor in factors.items():
        out[name] = (out[name] * factor).astype(out[name].dtype)
    return out
```

```python
import concourse.bass as bass
from concourse import mybir
from contextlib import ExitStack

F32 = mybir.dt.float32
BF16 = mybir.dt.bfloat16
U32 = mybir.dt.uint32
ALU = mybir.AluOpType
ACT = mybir.ActivationFunctionType
AX = mybir.AxisListType

P = 128
NH = 12
DK = 64
NP = NH // 2
TAPS = 4
I = 352
QB = 16
BLK = 32
NBL = P // BLK


def steps_of_a_batch():
    s = [("XN", 0), ("ZB", 0), ("GC", 0)]
    s += [("DD", d) for d in range(6)]
    s += [("QK", 0)]
    for p in range(1, NP):
        s += [("QK", p), ("SS", p - 1)]
    s += [("VP", 0), ("SS", NP - 1), ("CJ", 0), ("VP", 1)]
    s += [("GR", h) for h in range(NH)]
    s += [("LANES", 0), ("KT", 0), ("KT", 1)]
    s += [("VP", c) for c in range(2, 6)]
    s += [("XQ", 0), ("FU", 0), ("FU", 1), ("HQ", 0), ("GP", 0), ("GP", 1), ("HT", 0), ("HT", 1)]
    for k in range(NH + 7):
        s += [("SLOT", k)]
        if k in (14, 15, 16, 17):
            s += [("GP", k - 12)]
    s += [("OS", 0)]
    for c in range(6):
        s += [("OT", c)]
        if c:
            s += [("WO", c - 1)]
    s += [("WO", 5)]
    return s


RING = ("XN", "ZB", "GC", "DD", "QK", "GR", "KT", "VP", "GP", "XQ", "FU", "HT", "OT")
TAKES = {"FU": 2}


def ring_plan(steps):
    uses, n, count = {}, 0, [0] * 4
    for kind, a in steps:
        if kind in RING:
            for j in range(TAKES.get(kind, 1)):
                uses[kind, a, j] = (n % 4, count[n % 4])
                count[n % 4] += 1
                n += 1
    return uses, count


def build(nc, x, Wq, Wk, Wv, Wg, Wo, conv_q, conv_k, conv_v, Wgk, Wb, b_b, A_log, dt_bias, gnorm,
          w_gate, w_up, w_down, out, NB):
    T = x.shape[1]
    NT = T // P
    NU = NT * NH
    KD, VD = NH * DK, NH * P
    assert NT == 2 and x.shape[2] == P

    steps = steps_of_a_batch()
    ring, ring_uses = ring_plan(steps)

    ctx = ExitStack()
    with ctx:
        def sb(name, shape, dt=F32):
            return ctx.enter_context(nc.sbuf_tensor(name, shape, dt))

        def sem(name):
            return ctx.enter_context(nc.semaphore(name))

        wqk = sb("wqk", [P, TAPS, 2, KD])
        wv = sb("wv", [P, TAPS, VD])
        wg = sb("wg", [P, VD])
        wo = sb("wo", [P, NH, P])
        wzb = sb("wzb", [P, 2 * NH])
        zbias = sb("zbias", [P, 2 * NH])
        negA = sb("negA", [P, NH])
        gw = sb("gw", [P, 1])
        wgu = sb("wgu", [P, 2, I])
        wd = sb("wd", [P, 3, P])
        ident = sb("ident", [P, P])
        ones = sb("ones", [P, P])
        mle = sb("mle", [P, P])
        mgt = sb("mgt", [P, P])
        identb = sb("identb", [P, P], BF16)
        negm = sb("negm", [P, 4, P], BF16)
        pairsel = sb("pairsel", [P, 2])
        id32 = sb("id32", [P, BLK, BLK])
        mhalf = sb("mhalf", [P, 2 * NU])
        phalf = sb("phalf", [P, NU])

        xin = sb("xin", [P, NT, P])
        xres = sb("xres", [P, NT, P])
        xn = sb("xn", [P, NT, P])
        xnT = sb("xnT", [P, TAPS - 1 + T])
        stats = sb("stats", [P, NT, 6])
        mv = sb("mv", [P, NT, 2])
        veps = sb("veps", [P, NT])
        rstd = sb("rstd", [P, NT])
        z = sb("z", [P, NT, 2 * NH])
        nabs = sb("nabs", [P, NT, NH])
        ez = sb("ez", [P, NT, NH])
        lz = sb("lz", [P, NT, NH])
        eb = sb("eb", [P, NT, NH])
        sp = sb("sp", [P, NT, NH])
        eb1 = sb("eb1", [P, NT, NH])
        beta = sb("beta", [P, NT, NH])
        g = sb("g", [P, NT, NH])
        eGR = sb("eGR", [P, 2, NU])
        negG = sb("negG", [P, NU])
        sse = sb("sse", [P, 2, NT, NH])
        rinv = sb("rinv", [P, NU])
        cj = sb("cj", [P, NU])
        sqk = sb("sqk", [P, NU])
        bq = sb("bq", [P, NU])
        kr = sb("kr", [P, NH])
        gm = sb("gm", [P, 2, 4, P])
        KQ = sb("KQ", [P, NP, 2, T])
        sq = sb("sq", [P, 2, 2, T])
        UP = sb("UP", [P, NU, 2, P])
        Kt = sb("Kt", [P, NH, DK])
        V = sb("V", [P, NT, NH, P])
        Gt = sb("Gt", [P, NT, NH, P])
        XT = sb("XT", [P, NU, P])
        Xr = sb("Xr", [P, 2, NT, P])
        laneA = sb("laneA", [96, BLK, BLK])
        laneX = sb("laneX", [96, BLK, BLK])
        laneT = sb("laneT", [96, BLK, BLK])
        Wm = sb("Wm", [P, 2, NT, 2, P])
        W2 = sb("W2", [P, 2, NT, DK])
        eps0 = sb("eps0", [P, 6, P])
        eps1 = sb("eps1", [P, 2, P])
        Sb = sb("Sb", [P, 2, P])
        qse = sb("qse", [P, 4, P])
        ssO = sb("ssO", [P, NU])
        junk = sb("junk", [P, P])
        ov = sb("ov", [P, NU])
        rO = sb("rO", [P, NU])
        otb = sb("otb", [P, 2, 4, P])
        yb = sb("yb", [P, NT, P])
        NQ = NT * I
        qv = sb("qv", [P, NQ])
        qc = sb("qc", [P, NQ])
        qt = otb[:, :, :, :].rearrange("p a b c -> p (a b c)")
        qm = sb("qm", [P, NQ // QB])
        qs = sb("qs", [P, NQ // QB])
        qr = sb("qr", [P, NQ // QB])
        xq = sb("xq", [P, NT, P])
        xqT = sb("xqT", [P, T])
        hs = sb("hs", [P, NT, I])
        hT = sb("hT", [P, 3, NT, P])

        R = [ctx.enter_context(nc.psum_tensor(f"ring{b}", [P, 512], F32)) for b in range(4)]
        BW = ctx.enter_context(nc.psum_tensor("bank_w", [P, 512], F32))
        BF = ctx.enter_context(nc.psum_tensor("bank_f", [P, 512], F32))
        BE = ctx.enter_context(nc.psum_tensor("bank_e", [P, 512], F32))
        BO = ctx.enter_context(nc.psum_tensor("bank_o", [P, 512], F32))

        ring_full = [sem(f"ring_full{b}") for b in range(4)]
        ring_read = [sem(f"ring_read{b}") for b in range(4)]
        s_wload = sem("weights_loaded")
        s_wload2 = sem("weights_loaded2")
        s_setp = sem("pool_setup")
        s_setd = sem("vector_setup")
        s_seta = sem("scalar_setup")
        s_sett = sem("tensor_setup")
        s_setr = sem("vector_setup_read")
        s_x = sem("x_loaded")
        s_xused = sem("x_used")
        s_xres = sem("x_residual")
        s_var = sem("variance")
        s_rstd = sem("rstd")
        s_xn = sem("xn_ready")
        s_z = sem("z_ready")
        s_ez = sem("exps_of_z")
        s_g = sem("g_ready")
        s_gm = sem("gm_ready")
        s_sq = sem("squares_ready")
        s_ss = sem("square_sums")
        s_sse = sem("norms_ready")
        s_sqk = sem("key_norms")
        s_diag = sem("diagonals_written")
        s_lin = sem("lanes_loaded")
        s_lout = sem("lanes_written")
        s_solved = sem("lanes_solved")
        s_xt = sem("inverses_stored")
        s_zero = sem("diagonals_cleared")
        s_r0 = sem("scaled_values")
        s_xr = sem("inverse_turned")
        s_wa = sem("w_products")
        s_wr = sem("w_read")
        s_fb = sem("f_products")
        s_fr = sem("f_read")
        s_tt = sem("solve_matrix")
        s_be = sem("e_products")
        s_er = sem("e_read")
        s_bo = sem("o_products")
        s_or = sem("o_read")
        s_r1 = sem("r1_ready")
        s_osum = sem("output_squares")
        s_ov = sem("output_variance")
        s_ro = sem("output_rstd")
        s_og = sem("gated_outputs")
        s_xqs = sem("x_quantised")
        s_hq = sem("h_quantised")
        s_gate = sem("gate_silu")
        s_y = sem("y_products")
        s_yr = sem("y_read")
        s_yb = sem("y_stored_in_sbuf")
        s_out = sem("output_written")
        s_ach = sem("scalar_chain")
        s_dch = sem("vector_chain")
        s_pch = sem("pool_chain")
        s_held = sem("held")

        def cnt(i, per, n):
            return i * per + n

        def hold(eng):
            eng.sem_inc(s_held, 1)

        def zero(i):
            return isinstance(i, int) and i == 0

        def full(kind, a, j=0):
            return ring_full[ring[kind, a, j][0]]

        def read(kind, a, j=0):
            return ring_read[ring[kind, a, j][0]]

        def rv(i, kind, a, j=0):
            b, n = ring[kind, a, j]
            return i * ring_uses[b] + n + 1

        def bank(kind, a, j=0):
            return R[ring[kind, a, j][0]]

        def bc(ap, axis, n):
            v = ap.unsqueeze(axis)
            shape = list(v.shape)
            shape[axis] = n
            return v.broadcast_to(shape)

        def krows(h):
            return slice(DK * (h % 2), DK * (h % 2) + DK)

        def stage(k, lag):
            h = k - lag
            return h if 0 <= h < NH else None

        E_SLOTS = list(range(3, NH + 6))
        O_SLOTS = list(range(5, NH + 7))
        F_SLOTS = list(range(1, NH + 2))

        x_v = x.rearrange("b (t p) d -> b p t d", p=P)
        out_v = out.rearrange("b (t p) d -> b p t d", p=P)

        to_lanes = nc.dram_tensor("to_lanes", [NBL, NU, BLK, BLK], F32, kind="Internal").ap()
        from_lanes = nc.dram_tensor("from_lanes", [NBL, NU, BLK, BLK], F32, kind="Internal").ap()

        block = ctx.enter_context(nc.Block())

        @block.sync
        def _(sp):
            with nc.allow_non_contiguous_dma(reason="weights are laid out once"):
                sp.dma_start(V[:, 0, 0:NP, :].rearrange("p a b -> p (a b)"), Wk).then_inc(s_wload, 16)
                sp.dma_start(V[:, 0, NP:NH, :].rearrange("p a b -> p (a b)"), Wq).then_inc(s_wload, 16)
                sp.dma_start(Gt[:, 0, :, :].rearrange("p a b -> p (a b)"), Wv).then_inc(s_wload, 16)
                sp.dma_start(wg[:, :], Wg).then_inc(s_wload, 16)
                sp.dma_start(wo[:, :, :], Wo.rearrange("(h d) n -> d h n", d=P)).then_inc(s_wload, 16)
                sp.dma_start(wzb[:, 0:NH], Wgk).then_inc(s_wload, 16)
                sp.dma_start(wzb[:, NH:2 * NH], Wb).then_inc(s_wload, 16)
                sp.dma_start(zbias[:, 0:NH], dt_bias.partition_broadcast(P)).then_inc(s_wload, 16)
                sp.dma_start(zbias[:, NH:2 * NH], b_b.partition_broadcast(P)).then_inc(s_wload, 16)
                sp.dma_start(negA[:, :], A_log.partition_broadcast(P)).then_inc(s_wload, 16)
                sp.dma_start(gw[:, :], gnorm.unsqueeze(1)).then_inc(s_wload, 16)
                upf = UP[:, :, :, :].rearrange("p a b c -> p (a b c)")
                cvk = upf[:, 0:KD * TAPS]
                cvq = upf[:, KD * TAPS:2 * KD * TAPS]
                sp.dma_start(cvk, conv_k.rearrange("c t -> (c t)").partition_broadcast(P)).then_inc(s_wload, 16)
                sp.dma_start(cvq, conv_q.rearrange("c t -> (c t)").partition_broadcast(P)).then_inc(s_wload, 16)
                sp.wait_ge(s_setp, 1)
                hsf = hs[:, :, :].rearrange("p t i -> p (t i)")
                for n, w in enumerate((w_gate, w_up)):
                    dst = XT[:, 3 * n:3 * n + 3, :]
                    sp.dma_start(dst[:, 0:2, :], w[0:2 * P, :].rearrange("(c p) k -> p c k", p=P)).then_inc(s_wload, 16)
                    sp.dma_start(dst[0:I - 2 * P, 2, :], w[2 * P:I, :]).then_inc(s_wload, 16)
                sp.dma_start(hsf[:, 0:I], w_down).then_inc(s_wload, 16)
                sp.wait_ge(s_setr, 1)
                sp.dma_start(upf, conv_v.rearrange("c t -> (c t)").partition_broadcast(P)).then_inc(s_wload2, 16)

            def batch(i, first):
                for kind, a in steps:
                    if kind == "XN":
                        if not first:
                            sp.wait_ge(s_xused, cnt(i, 2, 0))
                        sp.dma_start(xin[:, :, :], x_v[i]).then_inc(s_x, 16)
                    if kind == "LANES":
                        sp.wait_ge(read("GR", NH - 1), rv(i, "GR", NH - 1))
                        for q in range(NBL):
                            r = slice(BLK * q, BLK * q + BLK)
                            sp.dma_start(to_lanes[q].rearrange("u j i -> j u i"), UP[r, :, 0, r]).then_inc(s_diag, 16)
                        sp.wait_ge(s_diag, i * 16 * NBL + 16 * NBL)
                        sp.dma_start(laneA[:, :, :].rearrange("l j i -> l (j i)"),
                                     to_lanes.rearrange("q u j i -> (q u) (j i)")).then_inc(s_lin, 16)
                        sp.wait_ge(s_solved, cnt(i, 1, 1))
                        sp.dma_start(from_lanes.rearrange("q u j i -> (q u) (j i)"),
                                     laneX[:, :, :].rearrange("l j i -> l (j i)")).then_inc(s_lout, 16)
                        sp.wait_ge(s_lout, i * 16 + 16)
                        for q in range(NBL):
                            r = slice(BLK * q, BLK * q + BLK)
                            sp.dma_start(XT[r, :, r], from_lanes[q].rearrange("u j i -> j u i")).then_inc(s_xt, 16)
                sp.wait_ge(s_yb, cnt(i, 1, 1))
                sp.dma_start(out_v[i], yb[:, :, :]).then_inc(s_out, 16)

            batch(0, True)
            if NB > 1:
                with sp.Fori(1, NB) as i:
                    batch(i, False)
            sp.wait_ge(s_out, 16 * NB)

        @block.gpsimd
        def _(pool):
            nc.gpsimd.memset(XT[:, :, :], 0.0).then_inc(s_setp, 1)
            nc.gpsimd.memset(ident[:, :], 0.0)
            nc.gpsimd.memset(ones[:, :], 1.0)
            nc.gpsimd.memset(negm[:, :, :], -30000.0)
            nc.gpsimd.memset(mhalf[:, :], -0.5)
            nc.gpsimd.memset(phalf[:, :], 0.5)
            nc.gpsimd.memset(id32[:, :, :], 0.0)
            nc.gpsimd.memset(pairsel[:, :], 1.0)
            nc.gpsimd.memset(xnT[:, 0:TAPS - 1], 0.0).then_inc(s_setp, 1)
            pool.wait_ge(s_setp, 2)
            nc.gpsimd.affine_select(out=ident[:, :], in_=ident[:, :], compare_op=ALU.not_equal, fill=1.0,
                                    base=0, pattern=[[-1, P]], channel_multiplier=1)
            nc.gpsimd.affine_select(out=mle[:, :], in_=ones[:, :], compare_op=ALU.is_ge, fill=0.0,
                                    base=0, pattern=[[1, P]], channel_multiplier=-1)
            nc.gpsimd.affine_select(out=mgt[:, :], in_=ones[:, :], compare_op=ALU.is_gt, fill=0.0,
                                    base=0, pattern=[[-1, P]], channel_multiplier=1)
            nc.gpsimd.affine_select(out=negm[:, :, :], in_=negm[:, :, :], compare_op=ALU.is_gt, fill=0.0,
                                    base=0, pattern=[[0, 4], [-1, P]], channel_multiplier=1)
            nc.gpsimd.affine_select(out=id32[:, :, :], in_=id32[:, :, :], compare_op=ALU.not_equal, fill=1.0,
                                    base=0, pattern=[[1, BLK], [-1, BLK]], channel_multiplier=0)
            nc.gpsimd.affine_select(out=pairsel[:, :], in_=pairsel[:, :], compare_op=ALU.is_ge, fill=0.0,
                                    base=0, pattern=[[-DK, 2]], channel_multiplier=1).then_inc(s_setp, 1)
            pool.wait_ge(s_setp, 3)
            nc.gpsimd.affine_select(out=pairsel[:, :], in_=pairsel[:, :], compare_op=ALU.is_gt, fill=0.0,
                                    base=DK, pattern=[[DK, 2]], channel_multiplier=-1)
            nc.gpsimd.tensor_copy(identb[:, :], ident[:, :]).then_inc(s_setp, 1)

            chain = [0, 0]

            def batch(i, base):
                chain[1] = 0

                def link(ins):
                    chain[1] += 1
                    ins.then_inc(s_pch, 1)
                    pool.wait_ge(s_pch, i * base + chain[1])

                for kind, a in steps:
                    if kind == "XN":
                        pool.wait_ge(s_var, cnt(i, 1, 1))
                        nc.gpsimd.tensor_tensor(out=rstd[:, :], in0=veps[:, :], in1=mhalf[:, 0:NT],
                                                op=ALU.pow).then_inc(s_rstd, 1)
                    if kind == "DD":
                        if a == 0:
                            pool.wait_ge(s_g, cnt(i, 1, 1))
                        if a >= 2:
                            pool.wait_ge(full("DD", a - 2), rv(i, "DD", a - 2))
                        elif not zero(i):
                            pool.wait_ge(full("DD", a + 4), rv(i - 1, "DD", a + 4))
                        gf = g[:, :, :].rearrange("p t h -> p (t h)")[:, 4 * a:4 * a + 4]
                        nc.gpsimd.tensor_tensor(out=gm[:, a % 2, :, :], in0=bc(gf, 2, P),
                                                in1=bc(mle[:, :], 1, 4), op=ALU.mult).then_inc(s_gm, 1)
                    if kind == "CJ":
                        pool.wait_ge(s_sse, cnt(i, 1, 1))
                        nc.gpsimd.tensor_tensor(out=sqk[:, :], in0=sse[:, 0, :, :].rearrange("p t h -> p (t h)"),
                                                in1=phalf[:, :], op=ALU.pow).then_inc(s_sqk, 1)
                    if kind == "LANES":
                        if not zero(i):
                            pool.wait_ge(s_lout, i * 16)
                            hold(pool)
                        link(nc.gpsimd.tensor_copy(laneX[:, :, :], id32[0:96, :, :]))
                        pool.wait_ge(s_lin, i * 16 + 16)
                        for j in range(BLK - 1):
                            n = BLK - 1 - j
                            t = laneT[:, 0:j + 1, 0:n]
                            link(nc.gpsimd.tensor_tensor(out=t, in0=laneX[:, 0:j + 1, j:j + 1].broadcast_to([96, j + 1, n]),
                                                         in1=laneA[:, j:j + 1, j + 1:BLK].broadcast_to([96, j + 1, n]),
                                                         op=ALU.mult))
                            w = laneX[:, 0:j + 1, j + 1:BLK]
                            ins = nc.gpsimd.tensor_tensor(out=w, in0=w, in1=t, op=ALU.subtract)
                            if j < BLK - 2:
                                link(ins)
                            else:
                                ins.then_inc(s_solved, 1)
                        for q in range(NBL):
                            r = slice(BLK * q, BLK * q + BLK)
                            hold(pool)
                            link(nc.gpsimd.memset(UP[r, :, 0, r], 0.0))
                        pool.sem_inc(s_zero, 1)
                    if kind == "OS":
                        pool.wait_ge(s_ov, cnt(i, 1, 1))
                        nc.gpsimd.tensor_tensor(out=rO[:, :], in0=ov[:, :], in1=mhalf[:, 0:NU],
                                                op=ALU.pow).then_inc(s_ro, 1)

            batch(0, 0)
            per = chain[1]
            if NB > 1:
                with pool.Fori(1, NB) as i:
                    batch(i, per)

        @block.scalar
        def _(act):
            act.wait_ge(s_wload, 16 * 18)
            nc.scalar.activation(negA[:, :], negA[:, :], ACT.Exp).then_inc(s_seta, 1)
            chain = [0]

            def batch(i, base):
                chain[0] = 0

                def link(ins):
                    chain[0] += 1
                    ins.then_inc(s_ach, 1)
                    act.wait_ge(s_ach, i * base + chain[0])

                for kind, a in steps:
                    b = bank(kind, a) if kind in RING else None
                    if kind in RING and kind not in ("ZB", "GR", "KT"):
                        act.wait_ge(full(kind, a), rv(i, kind, a))
                    if kind == "XN":
                        nc.scalar.activation(xnT[:, TAPS - 1:], b[:, 0:T], ACT.Copy).then_inc(read("XN", 0), 1)
                        if not zero(i):
                            act.wait_ge(s_yr, cnt(i, 2, 0))
                        nc.scalar.activation(xres[:, :, :], xin[:, :, :], ACT.Copy).then_inc(s_xused, 1)
                    if kind == "ZB":
                        act.wait_ge(s_z, cnt(i, 1, 1))
                        nc.scalar.activation(eb[:, :, :], z[:, :, NH:], ACT.Exp, scale=-1.0)
                        link(nc.scalar.activation(ez[:, :, :], nabs[:, :, :], ACT.Exp))
                        nc.scalar.activation(lz[:, :, :], ez[:, :, :], ACT.Ln, bias=1.0).then_inc(s_ez, 1)
                    if kind == "GC":
                        nc.scalar.activation(eGR[:, :, :].rearrange("p a u -> p (a u)"), b[:, 0:2 * NU],
                                             ACT.Exp).then_inc(read("GC", 0), 1)
                    if kind == "DD":
                        nc.scalar.activation(UP[:, 4 * a:4 * a + 4, 1, :], b[:, :], ACT.Exp)\
                          .then_inc(read("DD", a), 1)
                    if kind == "QK":
                        nc.scalar.activation(KQ[:, a, :, :].rearrange("p k t -> p (k t)"), b[:, :], ACT.Silu)\
                          .then_inc(read("QK", a), 1)
                        act.wait_ge(read("QK", a), rv(i, "QK", a))
                        if a >= 2:
                            act.wait_ge(s_ss, cnt(i, NP, a - 1))
                        nc.scalar.activation(sq[:, a % 2, :, :], KQ[:, a, :, :], ACT.Square).then_inc(s_sq, 1)
                    if kind in ("VP", "GP"):
                        t, q = a % 2, a // 2
                        dst = (V if kind == "VP" else Gt)[:, t, 4 * q:4 * q + 4, :]
                        nc.scalar.activation(dst, b[:, :], ACT.Silu).then_inc(read(kind, a), 1)
                    if kind == "XQ":
                        nc.scalar.activation(xqT[:, :], b[:, 0:T], ACT.Copy).then_inc(read("XQ", 0), 1)
                    if kind == "FU":
                        nc.scalar.activation(hs[:, a, :], b[:, 0:I], ACT.Silu).then_inc(read("FU", a, 0), 1)
                    if kind == "HT":
                        for c in range(3):
                            m = min(P, I - c * P)
                            ins = nc.scalar.activation(hT[0:m, c, a, :], b[0:m, c * P:c * P + P], ACT.Copy)
                        ins.then_inc(read("HT", a), 1)
                    if kind == "SLOT":
                        h = stage(a, 0)
                        if h is not None:
                            act.wait_ge(s_wa, cnt(i, NH, h + 1))
                            nc.scalar.activation(Wm[:, h % 2, :, :, :].rearrange("p t w n -> p (t w n)"), BW[:, :],
                                                 ACT.Copy).then_inc(s_wr, 1)
                        if a in E_SLOTS:
                            act.wait_ge(s_be, cnt(i, len(E_SLOTS), E_SLOTS.index(a) + 1))
                            h = stage(a, 3)
                            if h is not None:
                                ins = nc.scalar.activation(eps0[:, h % 6, :], BE[:, 0:P], ACT.Copy)
                            h = stage(a, 4)
                            if h is not None:
                                ins = nc.scalar.activation(Sb[krows(h), h % 2, :], BE[krows(h), P:2 * P], ACT.Copy)
                            h = stage(a, 6)
                            if h is not None:
                                ins = nc.scalar.activation(eps1[:, h % 2, :], BE[:, 2 * P:3 * P], ACT.Copy)
                            ins.then_inc(s_er, 1)
                        h = stage(a, 8)
                        if h is not None:
                            out_squares(i, h, base, link)
                    if kind == "OS":
                        for h in range(NH + 7 - 8, NH):
                            out_squares(i, h, base, link)
                    if kind == "OT":
                        nc.scalar.activation(otb[:, a % 2, :, :], b[:, :], ACT.Copy).then_inc(read("OT", a), 1)

            def out_squares(i, h, base, link):
                act.wait_ge(s_or, cnt(i, len(O_SLOTS), O_SLOTS.index(h + 7) + 1))
                for t in range(NT):
                    u = t * NH + h
                    link(nc.scalar.activation(junk[:, :], V[:, t, h, :], ACT.Square,
                                              accum_out=ssO[:, u:u + 1]))
                act.sem_inc(s_osum, 1)

            batch(0, 0)
            per = chain[0]
            if NB > 1:
                with act.Fori(1, NB) as i:
                    batch(i, per)

        @block.vector
        def _(dve):
            total = [0]

            def setup_link(ins):
                total[0] += 1
                ins.then_inc(s_dch, 1)
                dve.wait_ge(s_dch, total[0])

            def quantise(dst, src, n, link):
                nb = n // QB
                v, c, tt = qv[:, 0:n], qc[:, 0:n], qt[:, 0:n]
                by = lambda ap: ap.rearrange("p (b e) -> p b e", e=QB)
                link(nc.vector.tensor_reduce(qm[:, 0:nb], by(src), AX.X, ALU.max, apply_absolute_value=True))
                link(nc.vector.tensor_scalar(qs[:, 0:nb], qm[:, 0:nb], 1.0 / 6.0, 1e-12, ALU.mult, ALU.max))
                link(nc.vector.reciprocal(qr[:, 0:nb], qs[:, 0:nb]))
                link(nc.vector.tensor_tensor(by(v), by(src), bc(qr[:, 0:nb], 2, QB), ALU.mult))
                link(nc.vector.tensor_scalar(v.bitcast(U32), v.bitcast(U32), 0x7FFFFFFF, None, ALU.bitwise_and))
                link(nc.vector.tensor_scalar(c, v, 5.0, 2.0, ALU.is_gt, ALU.mult))
                link(nc.vector.scalar_tensor_tensor(c, v, 3.5, c, ALU.is_gt, ALU.add))
                link(nc.vector.scalar_tensor_tensor(c, v, 2.5, c, ALU.is_gt, ALU.add))
                link(nc.vector.tensor_scalar(tt, v, 1.75, None, ALU.is_gt))
                link(nc.vector.scalar_tensor_tensor(c, c, 2.0, tt, ALU.mult, ALU.add))
                for m in (1.25, 0.75, 0.25):
                    link(nc.vector.scalar_tensor_tensor(c, v, m, c, ALU.is_gt, ALU.add))
                link(nc.vector.scalar_tensor_tensor(v.bitcast(U32), src.bitcast(U32), 0x80000000, c.bitcast(U32),
                                                    ALU.bitwise_and, ALU.bitwise_or))
                link(nc.vector.tensor_scalar(qm[:, 0:nb], qs[:, 0:nb], 0.5, None, ALU.mult))
                return nc.vector.tensor_tensor(by(dst), by(v), bc(qm[:, 0:nb], 2, QB), ALU.mult)

            dve.wait_ge(s_wload, 16 * 18)
            dve.wait_ge(s_setp, 4)
            upf = UP[:, :, :, :].rearrange("p a b c -> p (a b c)")
            for w in range(2):
                base = V[:, 0, NP * w:NP * w + NP, :].rearrange("p a b -> p (a b)")
                cv = upf[:, w * KD * TAPS:(w + 1) * KD * TAPS].rearrange("p (c t) -> p c t", t=TAPS)
                for tap in range(TAPS):
                    ins = nc.vector.tensor_tensor(wqk[:, tap, w, :], base, cv[:, :, tap], ALU.mult)
            ins.then_inc(s_setr, 1)
            nc.vector.tensor_scalar(wo[:, :, :], wo[:, :, :], gw[:, 0:1], None, ALU.mult)
            for n in range(2):
                src = XT[:, 3 * n:3 * n + 3, :].rearrange("p c k -> p (c k)")
                setup_link(quantise(src, src, 3 * P, setup_link))
            dn = hs[:, :, :].rearrange("p t i -> p (t i)")[:, 0:I]
            setup_link(quantise(dn, dn, I, setup_link))
            dve.wait_ge(s_seta, 1)
            nc.vector.tensor_scalar(negA[:, :], negA[:, :], -1.0, None, ALU.mult).then_inc(s_setd, 1)
            dve.wait_ge(s_wload2, 16)
            cv = upf.rearrange("p (c t) -> p c t", t=TAPS)
            for tap in range(TAPS):
                ins = nc.vector.tensor_tensor(wv[:, tap, :], Gt[:, 0, :, :].rearrange("p a b -> p (a b)"),
                                              cv[:, :, tap], ALU.mult)
            dve.wait_ge(s_sett, 1)
            nc.vector.tensor_copy(wgu[:, 0, :], BW[:, 0:I])
            nc.vector.tensor_copy(wgu[:, 1, :], BF[:, 0:I])
            nc.vector.tensor_copy(wd[:, 0:2, :], BE[:, 0:2 * P])
            nc.vector.tensor_copy(wd[0:I - 2 * P, 2, :], BE[0:I - 2 * P, 2 * P:3 * P])
            setup_link(nc.vector.memset(XT[:, 0:6, :], 0.0))
            dve.sem_inc(s_setd, 1)
            chain = [0]

            def batch(i, per):
                chain[0] = total[0]

                def link(ins):
                    chain[0] += 1
                    ins.then_inc(s_dch, 1)
                    dve.wait_ge(s_dch, i * per + chain[0])

                for kind, a in steps:
                    b = bank(kind, a) if kind in RING else None
                    if kind == "XN":
                        dve.wait_ge(s_x, i * 16 + 16)
                        for t in range(NT):
                            link(nc.vector.bn_stats(stats[:, t, :], xin[:, t, :]))
                            hold(dve)
                            link(nc.vector.bn_aggr(mv[:, t, :], stats[:, t, :]))
                        nc.vector.tensor_scalar(veps[:, :], mv[:, :, 1], 1e-5, None, ALU.add).then_inc(s_var, 1)
                        dve.wait_ge(s_rstd, cnt(i, 1, 1))
                        for t in range(NT):
                            ins = nc.vector.tensor_scalar(xn[:, t, :], xin[:, t, :], mv[:, t, 0:1], rstd[:, t:t + 1],
                                                          ALU.subtract, ALU.mult)
                        link(ins)
                        dve.sem_inc(s_xn, 1)
                        dve.sem_inc(s_xused, 1)
                    if kind == "ZB":
                        dve.wait_ge(full("ZB", 0), rv(i, "ZB", 0))
                        link(nc.vector.tensor_tensor(z[:, :, :], b[:, 0:4 * NH].rearrange("p (t n) -> p t n", t=NT),
                                                     bc(zbias[:, :], 1, NT), ALU.add))
                        dve.sem_inc(read("ZB", 0), 1)
                        link(nc.vector.tensor_scalar(nabs[:, :, :].bitcast(U32), z[:, :, 0:NH].bitcast(U32), 0x80000000, None,
                                                     ALU.bitwise_or))
                        dve.sem_inc(s_z, 1)
                        dve.wait_ge(s_ez, cnt(i, 1, 1))
                        link(nc.vector.scalar_tensor_tensor(sp[:, :, :], z[:, :, 0:NH], 0.0, lz[:, :, :],
                                                            ALU.max, ALU.add))
                        link(nc.vector.tensor_tensor(g[:, :, :], sp[:, :, :], bc(negA[:, :], 1, NT), ALU.mult))
                        dve.sem_inc(s_g, 1)
                        link(nc.vector.tensor_scalar(eb1[:, :, :], eb[:, :, :], 1.0, None, ALU.add))
                        link(nc.vector.reciprocal(beta[:, :, :], eb1[:, :, :]))
                    if kind == "CJ":
                        dve.wait_ge(s_ss, cnt(i, NP, NP))
                        link(nc.vector.tensor_scalar(sse[:, :, :, :].rearrange("p k t h -> p (k t h)"), BE[:, 0:2 * NU],
                                                     1e-6, None, ALU.add))
                        dve.sem_inc(s_sse, 1)
                        sk = sse[:, 0, :, :].rearrange("p t h -> p (t h)")
                        link(nc.vector.reciprocal(rinv[:, :], sk))
                        link(nc.vector.tensor_tensor(cj[:, :], rinv[:, :], beta[:, :, :].rearrange("p t h -> p (t h)"),
                                                     ALU.mult))
                        link(nc.vector.tensor_scalar(bq[:, :], sse[:, 1, :, :].rearrange("p t h -> p (t h)"),
                                                     1e-5 * DK, None, ALU.mult))
                        dve.wait_ge(read("GC", 0), rv(i, "GC", 0))
                        link(nc.vector.tensor_scalar(negG[:, :], eGR[:, 0, :], -1.0, None, ALU.mult))
                        link(nc.vector.tensor_tensor(kr[:, :], cj[:, 0:NH], eGR[:, 1, 0:NH], ALU.mult))
                    if kind == "GR":
                        dve.wait_ge(full("GR", a), rv(i, "GR", a))
                        dve.wait_ge(read("DD", 5), rv(i, "DD", 5))
                        for t in range(NT):
                            u = t * NH + a
                            ins = nc.vector.scalar_tensor_tensor(
                                UP[:, u, :, :], b[:, t * 2 * P:(t + 1) * 2 * P].rearrange("p (k n) -> p k n", k=2),
                                cj[:, u:u + 1], bc(UP[:, u, 1, :], 1, 2), ALU.mult, ALU.mult)
                        ins.then_inc(read("GR", a), 1)
                    if kind == "KT":
                        dve.wait_ge(full("KT", a), rv(i, "KT", a))
                        h0 = NP * a
                        nc.vector.tensor_tensor(Kt[:, h0:h0 + NP, :],
                                                b[:, 0:NP * DK].rearrange("p (h d) -> p h d", d=DK),
                                                bc(kr[:, h0:h0 + NP], 2, DK), ALU.mult).then_inc(read("KT", a), 1)
                    if kind == "VP" and a == 5:
                        dve.wait_ge(s_sqk, cnt(i, 1, 1))
                        for c in range(6):
                            t, q = c % 2, c // 2
                            dve.wait_ge(read("VP", c), rv(i, "VP", c))
                            v = V[:, t, 4 * q:4 * q + 4, :]
                            u = t * NH + 4 * q
                            ins = nc.vector.tensor_tensor(v, v, bc(sqk[:, u:u + 4], 2, P), ALU.mult)
                        link(ins)
                        dve.sem_inc(s_r0, 1)
                        xnf = xn[:, :, :].rearrange("p t d -> p (t d)")
                        link(quantise(xq[:, :, :].rearrange("p t d -> p (t d)"), xnf, NT * P, link))
                        dve.sem_inc(s_xqs, 1)
                    if kind == "FU":
                        dve.wait_ge(read("FU", a, 0), rv(i, "FU", a, 0))
                        dve.wait_ge(full("FU", a, 1), rv(i, "FU", a, 1))
                        nc.vector.tensor_tensor(hs[:, a, :], hs[:, a, :], bank("FU", a, 1)[:, 0:I], ALU.mult)\
                          .then_inc(read("FU", a, 1), 1)
                    if kind == "HQ":
                        hf = hs[:, :, :].rearrange("p t i -> p (t i)")
                        dve.wait_ge(read("FU", 1, 1), rv(i, "FU", 1, 1))
                        link(quantise(hf, hf, NQ, link))
                        dve.sem_inc(s_hq, 1)
                        dve.wait_ge(s_xt, i * 16 * NBL + 16 * NBL)
                        turn(i, 0)
                    if kind == "SLOT":
                        if 1 <= a + 1 < NH:
                            turn(i, a + 1)
                        if a in F_SLOTS:
                            dve.wait_ge(s_fb, cnt(i, len(F_SLOTS), F_SLOTS.index(a) + 1))
                            h = stage(a, 1)
                            if h is not None:
                                nc.vector.tensor_copy(W2[DK:P, h % 2, :, :], BF[DK:P, 2 * P:3 * P]
                                                      .rearrange("p (t n) -> p t n", t=NT))
                                ins = nc.vector.tensor_tensor(
                                    UP[:, h::NH, 0, :], XT[:, h::NH, :],
                                    BF[:, 0:2 * P].rearrange("p (t n) -> p t n", t=NT), ALU.subtract)
                            h = stage(a, 2)
                            if h is not None:
                                tu = UP[0:DK, h::NH, 0, DK:P]
                                ins = nc.vector.tensor_tensor(tu, tu, BF[0:DK, 3 * P:4 * P]
                                                              .rearrange("p (t n) -> p t n", t=NT), ALU.add)
                            ins.then_inc(s_fr, 1)
                        if a in O_SLOTS:
                            dve.wait_ge(s_bo, cnt(i, len(O_SLOTS), O_SLOTS.index(a) + 1))
                            h = stage(a, 5)
                            if h is not None:
                                u = NH + h
                                v1 = V[:, 1, h, :]
                                nc.vector.scalar_tensor_tensor(v1, BO[:, 0:P], negG[:, u:u + 1], v1, ALU.mult, ALU.add)\
                                  .then_inc(s_r1, 1)
                                link(nc.vector.tensor_scalar(qse[:, h % 4, :], BO[:, P:2 * P], eGR[:, 0, u:u + 1], None,
                                                             ALU.mult))
                            h = stage(a, 7)
                            if h is not None:
                                nc.vector.tensor_copy(V[:, 0, h, :], BO[:, 2 * P:3 * P])
                                link(nc.vector.tensor_tensor(V[:, 1, h, :], BO[:, 3 * P:4 * P], qse[:, h % 4, :],
                                                             ALU.add))
                            dve.sem_inc(s_or, 1)
                    if kind == "OS":
                        dve.wait_ge(s_osum, cnt(i, NH, NH))
                        link(nc.vector.scalar_tensor_tensor(ov[:, :], ssO[:, :], 1.0 / P, bq[:, :], ALU.mult, ALU.add))
                        dve.sem_inc(s_ov, 1)
                        dve.wait_ge(s_ro, cnt(i, 1, 1))
                        for c in range(6):
                            t, q = c // 3, c % 3
                            dve.wait_ge(read("GP", t + 2 * q), rv(i, "GP", t + 2 * q))
                            for h in range(4 * q, 4 * q + 4):
                                u = t * NH + h
                                v = V[:, t, h, :]
                                ins = nc.vector.scalar_tensor_tensor(v, v, rO[:, u:u + 1], Gt[:, t, h, :],
                                                                     ALU.mult, ALU.mult)
                            ins.then_inc(s_og, 1)
                    if kind == "WO" and a % 3 == 2:
                        t = a // 3
                        dve.wait_ge(s_y, cnt(i, 2, t + 1))
                        if t == 0 and not zero(i):
                            dve.wait_ge(s_out, i * 16)
                        if t == 0:
                            dve.wait_ge(s_xused, cnt(i, 2, 2))
                        ins = nc.vector.tensor_tensor(yb[:, t, :], (BW, BF)[t][:, 0:P], xres[:, t, :], ALU.add)
                        ins.then_inc(s_yr, 1)
                        if t == 1:
                            dve.wait_ge(s_yr, cnt(i, 2, 2))
                            dve.sem_inc(s_yb, 1)

            def turn(i, h):
                if h >= 2:
                    dve.wait_ge(s_wa, cnt(i, NH, h - 1))
                for t in range(NT):
                    ins = nc.vector.transpose(Xr[:, h % 2, t, :], XT[:, t * NH + h, :])
                ins.then_inc(s_xr, 1)

            batch(0, 0)
            per = chain[0] - total[0]
            if NB > 1:
                with dve.Fori(1, NB) as i:
                    batch(i, per)

        @block.tensor
        def _(pe):
            mm = nc.tensor.matmul
            pe.wait_ge(s_setp, 4)
            pe.wait_ge(s_setd, 1)
            for n, b in enumerate((BW, BF)):
                for c in range(3):
                    m = min(P, I - c * P)
                    ins = nc.tensor.transpose(b[:, c * P:c * P + m], XT[0:m, 3 * n + c, :], ident[0:m, 0:m])
            dn = hs[:, :, :].rearrange("p t i -> p (t i)")
            for c in range(3):
                m = min(P, I - c * P)
                ins = nc.tensor.transpose(BE[0:m, c * P:c * P + P], dn[:, c * P:c * P + m], ident[:, :])
            ins.then_inc(s_sett, 1)
            pe.wait_ge(s_setd, 2)

            def batch(i, first):
                def take(kind, a, j=0):
                    b, n = ring[kind, a, j]
                    if n or not first:
                        pe.wait_ge(ring_read[b], i * ring_uses[b] + n)
                    return R[b]

                for kind, a in steps:
                    if kind == "XN":
                        b = take("XN", 0)
                        pe.wait_ge(s_xn, cnt(i, 1, 1))
                        for t in range(NT):
                            ins = nc.tensor.transpose(b[:, t * P:t * P + P], xn[:, t, :], ident[:, :])
                        ins.then_inc(full("XN", 0), 1)
                    if kind == "ZB":
                        b = take("ZB", 0)
                        pe.wait_ge(read("XN", 0), rv(i, "XN", 0))
                        for t in range(NT):
                            o = TAPS - 1 + t * P
                            ins = mm(b[:, t * 2 * NH:(t + 1) * 2 * NH], xnT[:, o:o + P], wzb[:, :], start=True, stop=True)
                        ins.then_inc(full("ZB", 0), 1)
                    if kind == "GC":
                        b = take("GC", 0)
                        pe.wait_ge(s_g, cnt(i, 1, 1))
                        gf = g[:, :, :].rearrange("p t h -> p (t h)")
                        mm(b[:, 0:NU], mle[:, :], gf, start=True, stop=True)
                        mm(b[:, NU:2 * NU], mgt[:, :], gf, start=True, stop=True).then_inc(full("GC", 0), 1)
                    if kind == "DD":
                        b = take("DD", a)
                        pe.wait_ge(s_gm, cnt(i, 6, a + 1))
                        mm(b[:, :], mgt[:, :], gm[:, a % 2, :, :].rearrange("p u n -> p (u n)"), start=True, stop=False)
                        mm(b[:, :], identb[:, :], negm[:, :, :].rearrange("p u n -> p (u n)"), start=False, stop=True)\
                            .then_inc(full("DD", a), 1)
                    if kind == "QK":
                        b = take("QK", a)
                        for w in range(2):
                            for tap in range(TAPS):
                                ins = mm(b[:, w * T:(w + 1) * T], wqk[:, tap, w, a * P:(a + 1) * P],
                                         xnT[:, tap:tap + T], start=(tap == 0), stop=(tap == TAPS - 1))
                        ins.then_inc(full("QK", a), 1)
                    if kind == "SS":
                        pe.wait_ge(s_sq, cnt(i, NP, a + 1))
                        for w in range(2):
                            for t in range(NT):
                                o = (w * NT + t) * NH + 2 * a
                                ins = mm(BE[:, o:o + 2], sq[:, a % 2, w, t * P:(t + 1) * P], pairsel[:, :],
                                         start=True, stop=True)
                        ins.then_inc(s_ss, 1)
                    if kind == "GR":
                        b = take("GR", a)
                        r, p = krows(a), a // 2
                        for t in range(NT):
                            ts = slice(t * P, t * P + P)
                            ins = mm(b[:, t * 2 * P:(t + 1) * 2 * P], KQ[r, p, 0, ts], KQ[r, p, :, ts],
                                     start=True, stop=True)
                        ins.then_inc(full("GR", a), 1)
                    if kind == "KT":
                        b = take("KT", a)
                        for n in range(3):
                            ins = nc.tensor.transpose(b[:, n * P:n * P + P], KQ[:, 3 * a + n, 0, 0:P], ident[:, :])
                        ins.then_inc(full("KT", a), 1)
                    if kind == "VP":
                        b = take("VP", a)
                        t, q = a % 2, a // 2
                        for tap in range(TAPS):
                            ins = mm(b[:, :], xnT[:, t * P + tap:t * P + tap + P], wv[:, tap, q * 512:(q + 1) * 512],
                                     start=(tap == 0), stop=(tap == TAPS - 1))
                        ins.then_inc(full("VP", a), 1)
                    if kind == "GP":
                        b = take("GP", a)
                        t, q = a % 2, a // 2
                        o = TAPS - 1 + t * P
                        mm(b[:, :], xnT[:, o:o + P], wg[:, q * 512:(q + 1) * 512], start=True, stop=True)\
                            .then_inc(full("GP", a), 1)
                    if kind == "XQ":
                        b = take("XQ", 0)
                        pe.wait_ge(s_xqs, cnt(i, 1, 1))
                        for t in range(NT):
                            ins = nc.tensor.transpose(b[:, t * P:t * P + P], xq[:, t, :], ident[:, :])
                        ins.then_inc(full("XQ", 0), 1)
                    if kind == "FU":
                        pe.wait_ge(read("XQ", 0), rv(i, "XQ", 0))
                        for j in range(2):
                            b = take("FU", a, j)
                            mm(b[:, 0:I], xqT[:, a * P:(a + 1) * P], wgu[:, j, :], start=True, stop=True)\
                                .then_inc(full("FU", a, j), 1)
                    if kind == "HT":
                        b = take("HT", a)
                        pe.wait_ge(s_hq, cnt(i, 1, 1))
                        for c in range(3):
                            m = min(P, I - c * P)
                            ins = nc.tensor.transpose(b[0:m, c * P:c * P + P], hs[:, a, c * P:c * P + m], ident[:, :])
                        ins.then_inc(full("HT", a), 1)
                    if kind == "SLOT":
                        h = stage(a, 0)
                        if h is not None:
                            if h == 0:
                                pe.wait_ge(s_zero, cnt(i, 1, 1))
                                if not first:
                                    pe.wait_ge(s_yr, cnt(i, 2, 0))
                            else:
                                pe.wait_ge(s_wr, cnt(i, NH, h))
                            pe.wait_ge(s_xr, cnt(i, NH, h + 1))
                            for t in range(NT):
                                u = t * NH + h
                                mm(BW[:, t * 2 * P:t * 2 * P + P], Xr[:, h % 2, t, :], UP[:, u, 0, :], start=True, stop=True)
                                ins = mm(BW[:, t * 2 * P + P:(t + 1) * 2 * P], UP[:, u, 0, :], Xr[:, h % 2, t, :],
                                         start=True, stop=True)
                            ins.then_inc(s_wa, 1)
                        if a in F_SLOTS:
                            n = F_SLOTS.index(a)
                            if n:
                                pe.wait_ge(s_fr, cnt(i, len(F_SLOTS), n))
                            h = stage(a, 1)
                            if h is not None:
                                pe.wait_ge(s_wr, cnt(i, NH, h + 1))
                                for t in range(NT):
                                    u = t * NH + h
                                    mm(BF[:, t * P:t * P + P], Wm[:, h % 2, t, 1, :], XT[:, u, :], start=True, stop=True)
                                    ins = mm(BF[DK:P, 2 * P + t * DK:2 * P + (t + 1) * DK], Wm[:, h % 2, t, 0, DK:P],
                                             Wm[:, h % 2, t, 1, 0:DK], start=True, stop=True)
                            h = stage(a, 2)
                            if h is not None:
                                hold(pe)
                                for t in range(NT):
                                    u = t * NH + h
                                    ins = mm(BF[0:DK, 3 * P + t * DK:3 * P + (t + 1) * DK], W2[DK:P, h % 2, t, :],
                                             UP[DK:P, u, 0, DK:P], start=True, stop=True)
                            ins.then_inc(s_fb, 1)
                        if a in E_SLOTS:
                            n = E_SLOTS.index(a)
                            if n:
                                pe.wait_ge(s_er, cnt(i, len(E_SLOTS), n))
                            h = stage(a, 3)
                            if h is not None:
                                if h == 0:
                                    pe.wait_ge(s_r0, cnt(i, 1, 1))
                                pe.wait_ge(s_fr, cnt(i, len(F_SLOTS), F_SLOTS.index(h + 2) + 1))
                                ins = mm(BE[:, 0:P], UP[:, h, 0, :], V[:, 0, h, :], start=True, stop=True)
                            h = stage(a, 4)
                            if h is not None:
                                if h == 0:
                                    pe.wait_ge(read("KT", 0), rv(i, "KT", 0))
                                    pe.wait_ge(read("KT", 1), rv(i, "KT", 1))
                                ins = mm(BE[krows(h), P:2 * P], Kt[:, h, :], eps0[:, h % 6, :], start=True, stop=True)
                            h = stage(a, 6)
                            if h is not None:
                                pe.wait_ge(s_r1, cnt(i, NH, h + 1))
                                ins = mm(BE[:, 2 * P:3 * P], UP[:, NH + h, 0, :], V[:, 1, h, :], start=True, stop=True)
                            ins.then_inc(s_be, 1)
                        if a in O_SLOTS:
                            n = O_SLOTS.index(a)
                            if n:
                                pe.wait_ge(s_or, cnt(i, len(O_SLOTS), n))
                            h = stage(a, 5)
                            if h is not None:
                                for w in range(2):
                                    ins = mm(BO[:, w * P:(w + 1) * P], KQ[krows(h), h // 2, w, P:2 * P], Sb[krows(h), h % 2, :],
                                             start=True, stop=True)
                            h = stage(a, 7)
                            if h is not None:
                                if a not in E_SLOTS:
                                    pe.wait_ge(s_er, cnt(i, len(E_SLOTS), len(E_SLOTS)))
                                for t in range(NT):
                                    e = eps0[:, h % 6, :] if t == 0 else eps1[:, h % 2, :]
                                    ins = mm(BO[:, (2 + t) * P:(3 + t) * P], UP[:, t * NH + h, 1, :], e,
                                             start=True, stop=True)
                            ins.then_inc(s_bo, 1)
                    if kind == "OT":
                        b = take("OT", a)
                        t, q = a // 3, a % 3
                        pe.wait_ge(s_og, cnt(i, 6, a + 1))
                        for n in range(4):
                            ins = nc.tensor.transpose(b[:, n * P:(n + 1) * P], V[:, t, 4 * q + n, :], ident[:, :])
                        ins.then_inc(full("OT", a), 1)
                    if kind == "WO":
                        t, q = a // 3, a % 3
                        y = (BW, BF)[t]
                        if q == 0:
                            if t == 0:
                                pe.wait_ge(read("HT", 0), rv(i, "HT", 0))
                                pe.wait_ge(read("HT", 1), rv(i, "HT", 1))
                            for c in range(3):
                                m = min(P, I - c * P)
                                mm(y[:, 0:P], hT[0:m, c, t, :], wd[0:m, c, :], start=(c == 0), stop=False)
                        pe.wait_ge(read("OT", a), rv(i, "OT", a))
                        for n in range(4):
                            h = 4 * q + n
                            ins = mm(y[:, 0:P], otb[:, a % 2, n, :], wo[:, h, :], start=False, stop=(h == NH - 1))
                        if q == 2:
                            ins.then_inc(s_y, 1)

            batch(0, True)
            if NB > 1:
                with pe.Fori(1, NB) as i:
                    batch(i, False)


_INS = ["L0_attn_hidden_states", "L0_attn_Wq", "L0_attn_Wk", "L0_attn_Wv", "L0_attn_Wg", "L0_attn_Wo",
        "L0_attn_conv_q", "L0_attn_conv_k", "L0_attn_conv_v", "L0_attn_Wgk", "L0_attn_Wb", "L0_attn_b_b",
        "L0_attn_A_log", "L0_attn_dt_bias", "L0_attn_g_norm_weight", "L0_ffn_w_gate", "L0_ffn_w_up",
        "L0_ffn_w_down"]


def kernel(**inputs):
    import numpy as _np
    import concourse.bacc as _bacc
    from concourse import mybir as _mybir
    from concourse.bass_utils import run_bass_kernel_spmd as _run

    nc = _bacc.Bacc("TRN2", target_bir_lowering=False, num_devices=1)
    arrays, args = {}, []
    for name in _INS:
        a = _np.ascontiguousarray(inputs[name])
        arrays[f"in_{name}_dram"] = a
        args.append(nc.dram_tensor(f"in_{name}_dram", a.shape, _mybir.dt.from_np(a.dtype), kind="ExternalInput").ap())
    shape = inputs["L0_attn_hidden_states"].shape
    o = nc.dram_tensor("out_0_dram", shape, _mybir.dt.from_np(_np.dtype("float32")), kind="ExternalOutput").ap()
    build(nc, *args, o, shape[0])
    r = _run(nc, [arrays], core_ids=[0])
    return r.results[0]["out_0_dram"]
```

```python
import concourse.bass as bass
from concourse import mybir
from contextlib import ExitStack

F32 = mybir.dt.float32
BF16 = mybir.dt.bfloat16
U32 = mybir.dt.uint32
ALU = mybir.AluOpType
ACT = mybir.ActivationFunctionType
AX = mybir.AxisListType

P = 128
NH = 12
DK = 64
NP = NH // 2
TAPS = 4
I = 352
QB = 16
BLK = 32
NBL = P // BLK


BETWEEN = {0: [("XN", 0)], 2: [("ZB", 0)], 4: [("GC", 0)], 5: [("QK", 0)], 6: [("SS", 0)],
           7: [("QK", 1)], 8: [("SS", 1)], 9: [("QK", 2)], 10: [("SS", 2)], 11: [("QK", 3)],
           12: [("SS", 3)], 13: [("QK", 4)], 14: [("SS", 4)], 15: [("QK", 5)], 16: [("SS", 5), ("DD", 0)],
           17: [("DD", 3), ("DD", 1)], 18: [("DD", 4), ("DD", 2), ("DD", 5)]}


def steps_of_an_iteration():
    s = []
    for k in range(NH + 7):
        s += [("SLOT", k, 0)] + [(kind, a, 1) for kind, a in BETWEEN.get(k, [])]
    s += [("OS", 0, 0), ("CJ", 0, 1)]
    s += [("GR", h, 1) for h in range(NH)]
    s += [("LANES", 0, 1), ("OG", 0, 0)]
    s += [("KT", 0, 1), ("KT", 1, 1), ("VP", 0, 1)]
    for c in range(6):
        s += [("OT", c, 0)]
        if c:
            s += [("WO", c - 1, 0)]
    s += [("WO", 5, 0)]
    for c in range(1, 6):
        s += [("VP", c, 1), ("VT", c - 1, 1)]
    s += [("GP", 0, 1), ("VT", 5, 1), ("XQ", 0, 1), ("GP", 1, 1), ("FU", 0, 1), ("FU", 1, 1)]
    s += [("GP", c, 1) for c in range(2, 6)]
    s += [("HQ", 0, 1), ("HT", 0, 1), ("HT", 1, 1)]
    return s


RING = ("XN", "ZB", "GC", "DD", "QK", "SS", "GR", "KT", "VP", "VT", "GP", "XQ", "FU", "HT")
TAKES = {"FU": 2}


def ring_plan(steps):
    uses, n, count = {}, 0, [0] * 4
    for kind, a, _ in steps:
        if kind in RING:
            for j in range(TAKES.get(kind, 1)):
                uses[kind, a, j] = (n % 4, count[n % 4])
                count[n % 4] += 1
                n += 1
    return uses, count


def build(nc, x, Wq, Wk, Wv, Wg, Wo, conv_q, conv_k, conv_v, Wgk, Wb, b_b, A_log, dt_bias, gnorm,
          w_gate, w_up, w_down, out, NB):
    T = x.shape[1]
    NT = T // P
    NU = NT * NH
    KD, VD = NH * DK, NH * P
    assert NT == 2 and x.shape[2] == P

    steps = steps_of_an_iteration()
    dds = [a for kind, a, _ in steps if kind == "DD"]
    ring, ring_uses = ring_plan(steps)

    ctx = ExitStack()
    with ctx:
        def sb(name, shape, dt=F32):
            return ctx.enter_context(nc.sbuf_tensor(name, shape, dt))

        def sem(name):
            return ctx.enter_context(nc.semaphore(name))

        wqk = sb("wqk", [P, 2, KD])
        wv = sb("wv", [P, VD])
        ckq = sb("ckq", [P, 2, NP, TAPS])
        cvv = sb("cvv", [P, NH, TAPS])
        wg = sb("wg", [P, VD])
        wo = sb("wo", [P, NH, P])
        wzb = sb("wzb", [P, 2 * NH])
        zbias = sb("zbias", [P, 2 * NH])
        negA = sb("negA", [P, NH])
        gw = sb("gw", [P, 1])
        wgu = sb("wgu", [P, 2, I])
        wd = sb("wd", [P, 3, P])
        ident = sb("ident", [P, P])
        ones = sb("ones", [P, P])
        mle = sb("mle", [P, P])
        mgt = sb("mgt", [P, P])
        identb = sb("identb", [P, P], BF16)
        negm = sb("negm", [P, 4, P], BF16)
        pairsel = sb("pairsel", [P, 2])
        id32 = sb("id32", [P, BLK, BLK])
        mhalf = sb("mhalf", [P, 2 * NU])
        phalf = sb("phalf", [P, NU])

        xin = sb("xin", [P, NT, P])
        xres = sb("xres", [P, NT, P])
        xn = sb("xn", [P, NT, P])
        xnT = sb("xnT", [P, T])
        stats = sb("stats", [P, NT, 6])
        mv = sb("mv", [P, NT, 2])
        veps = sb("veps", [P, NT])
        rstd = sb("rstd", [P, NT])
        z = sb("z", [P, NT, 2 * NH])
        nabs = sb("nabs", [P, NT, NH])
        ez = sb("ez", [P, NT, NH])
        lz = sb("lz", [P, NT, NH])
        eb = sb("eb", [P, NT, NH])
        sp = sb("sp", [P, NT, NH])
        eb1 = sb("eb1", [P, NT, NH])
        beta = sb("beta", [P, NT, NH])
        g = sb("g", [P, NT, NH])
        eGR = sb("eGR", [P, 2, NU])
        negG = sb("negG", [P, NU])
        sse = sb("sse", [P, 2, NT, NH])
        rinv = sb("rinv", [P, NU])
        cj = sb("cj", [P, NU])
        sqk = sb("sqk", [P, NU])
        bq = sb("bq", [P, NU])
        kr = sb("kr", [P, NH])
        gm = sb("gm", [P, 2, 4, P])
        KQ2 = sb("KQ2", [P, 2, NP, 2, T])
        sq = sb("sq", [P, 2, 2, T])
        vc = sb("vc", [P, 2, 2, T])
        eG = sb("eG", [P, NU])
        UP = sb("UP", [P, NU, 2, P])
        Kt = sb("Kt", [P, NH, DK])
        V = sb("V", [P, NT, NH, P])
        Gt = sb("Gt", [P, NT, NH, P])
        XT = sb("XT", [P, NU, P])
        Xr = sb("Xr", [P, 2, NT, P])
        laneA = sb("laneA", [96, BLK, BLK])
        laneX = sb("laneX", [96, BLK, BLK])
        laneT = sb("laneT", [96, BLK, BLK])
        Wm = sb("Wm", [P, 2, NT, 2, P])
        W2 = sb("W2", [P, 2, NT, DK])
        eps0 = sb("eps0", [P, 6, P])
        eps1 = sb("eps1", [P, 2, P])
        Sb = sb("Sb", [P, 2, P])
        qse = sb("qse", [P, 4, P])
        ssO = sb("ssO", [P, NU])
        junk = sb("junk", [P, P])
        ov = sb("ov", [P, NU])
        rO = sb("rO", [P, NU])
        otb = sb("otb", [P, 2, 4, P])
        yb = sb("yb", [P, NT, P])
        NQ = NT * I
        qv = sb("qv", [P, NQ])
        qc = sb("qc", [P, NQ])
        qt = otb[:, :, :, :].rearrange("p a b c -> p (a b c)")
        qm = sb("qm", [P, NQ // QB])
        qs = sb("qs", [P, NQ // QB])
        qr = sb("qr", [P, NQ // QB])
        xq = sb("xq", [P, NT, P])
        xqT = sb("xqT", [P, T])
        hs = sb("hs", [P, NT, I])
        hT = sb("hT", [P, 3, NT, P])

        R = [ctx.enter_context(nc.psum_tensor(f"ring{b}", [P, 512], F32)) for b in range(4)]
        BW = ctx.enter_context(nc.psum_tensor("bank_w", [P, 512], F32))
        BF = ctx.enter_context(nc.psum_tensor("bank_f", [P, 512], F32))
        BE = ctx.enter_context(nc.psum_tensor("bank_e", [P, 512], F32))
        BO = ctx.enter_context(nc.psum_tensor("bank_o", [P, 512], F32))

        ring_full = [sem(f"ring_full{b}") for b in range(4)]
        ring_read = [sem(f"ring_read{b}") for b in range(4)]
        s_wload = sem("weights_loaded")
        s_setp = sem("pool_setup")
        s_setd = sem("vector_setup")
        s_seta = sem("scalar_setup")
        s_sett = sem("tensor_setup")
        s_x = sem("x_loaded")
        s_xused = sem("x_used")
        s_xres = sem("x_residual")
        s_tap = sem("first_tap")
        s_kq = sem("keys_and_queries")
        s_vtap = sem("first_value_tap")
        s_vs = sem("values_silu")
        s_otf = sem("ot_products")
        s_otr = sem("ot_read")
        s_var = sem("variance")
        s_rstd = sem("rstd")
        s_xn = sem("xn_ready")
        s_z = sem("z_ready")
        s_ez = sem("exps_of_z")
        s_g = sem("g_ready")
        s_gm = sem("gm_ready")
        s_sq = sem("squares_ready")
        s_sqk = sem("key_norms")
        s_diag = sem("diagonals_written")
        s_lin = sem("lanes_loaded")
        s_lout = sem("lanes_written")
        s_solved = sem("lanes_solved")
        s_xt = sem("inverses_stored")
        s_zero = sem("diagonals_cleared")
        s_xr = sem("inverse_turned")
        s_wa = sem("w_products")
        s_wr = sem("w_read")
        s_fb = sem("f_products")
        s_fr = sem("f_read")
        s_tt = sem("solve_matrix")
        s_be = sem("e_products")
        s_er = sem("e_read")
        s_bo = sem("o_products")
        s_or = sem("o_read")
        s_r1 = sem("r1_ready")
        s_osum = sem("output_squares")
        s_ov = sem("output_variance")
        s_ro = sem("output_rstd")
        s_og = sem("gated_outputs")
        s_xqs = sem("x_quantised")
        s_hq = sem("h_quantised")
        s_gate = sem("gate_silu")
        s_y = sem("y_products")
        s_yr = sem("y_read")
        s_yb = sem("y_stored_in_sbuf")
        s_out = sem("output_written")
        s_ach = sem("scalar_chain")
        s_dch = sem("vector_chain")
        s_pch = sem("pool_chain")
        s_held = sem("held")

        def cnt(i, per, n):
            return i * per + n

        def hold(eng):
            eng.sem_inc(s_held, 1)

        def zero(i):
            return isinstance(i, int) and i == 0

        def full(kind, a, j=0):
            return ring_full[ring[kind, a, j][0]]

        def read(kind, a, j=0):
            return ring_read[ring[kind, a, j][0]]

        def rv(i, kind, a, j=0):
            b, n = ring[kind, a, j]
            return i * ring_uses[b] + n + 1

        def bank(kind, a, j=0):
            return R[ring[kind, a, j][0]]

        def of(it):
            for kind, a, off in steps:
                if isinstance(it, int) and not 0 <= it + off < NB:
                    continue
                yield kind, a, it + off

        parity = [0]

        def run(eng, iteration):
            for it in (-1, 0):
                parity[0] = it % 2
                iteration(it)
            with eng.Fori(1, NB - 2, 2) as it:
                for n in range(2):
                    parity[0] = (1 + n) % 2
                    iteration(it + n)
            parity[0] = (NB - 1) % 2
            iteration(NB - 1)

        def kq(off):
            return KQ2[:, (parity[0] + off) % 2, :, :, :]

        def bc(ap, axis, n):
            v = ap.unsqueeze(axis)
            shape = list(v.shape)
            shape[axis] = n
            return v.broadcast_to(shape)

        def krows(h):
            return slice(DK * (h % 2), DK * (h % 2) + DK)

        def stage(k, lag):
            h = k - lag
            return h if 0 <= h < NH else None

        E_SLOTS = list(range(3, NH + 6))
        O_SLOTS = list(range(5, NH + 7))
        F_SLOTS = list(range(1, NH + 2))

        x_v = x.rearrange("b (t p) d -> b p t d", p=P)
        out_v = out.rearrange("b (t p) d -> b p t d", p=P)

        to_lanes = nc.dram_tensor("to_lanes", [NBL, NU, BLK, BLK], F32, kind="Internal").ap()
        from_lanes = nc.dram_tensor("from_lanes", [NBL, NU, BLK, BLK], F32, kind="Internal").ap()

        block = ctx.enter_context(nc.Block())

        @block.sync
        def _(sp):
            with nc.allow_non_contiguous_dma(reason="weights are laid out once"):
                sp.dma_start(wqk[:, 0, :], Wk).then_inc(s_wload, 16)
                sp.dma_start(wqk[:, 1, :], Wq).then_inc(s_wload, 16)
                sp.dma_start(wv[:, :], Wv).then_inc(s_wload, 16)
                for n, c in enumerate((conv_k, conv_q)):
                    sp.dma_start(ckq[:, n, :, :], c.rearrange("(p c) t -> c p t", c=P)).then_inc(s_wload, 16)
                sp.dma_start(cvv[:, :, :], conv_v.rearrange("(h c) t -> c h t", c=P)).then_inc(s_wload, 16)
                sp.dma_start(wg[:, :], Wg).then_inc(s_wload, 16)
                sp.dma_start(wo[:, :, :], Wo.rearrange("(h d) n -> d h n", d=P)).then_inc(s_wload, 16)
                sp.dma_start(wzb[:, 0:NH], Wgk).then_inc(s_wload, 16)
                sp.dma_start(wzb[:, NH:2 * NH], Wb).then_inc(s_wload, 16)
                sp.dma_start(zbias[:, 0:NH], dt_bias.partition_broadcast(P)).then_inc(s_wload, 16)
                sp.dma_start(zbias[:, NH:2 * NH], b_b.partition_broadcast(P)).then_inc(s_wload, 16)
                sp.dma_start(negA[:, :], A_log.partition_broadcast(P)).then_inc(s_wload, 16)
                sp.dma_start(gw[:, :], gnorm.unsqueeze(1)).then_inc(s_wload, 16)
                sp.wait_ge(s_setp, 1)
                hsf = hs[:, :, :].rearrange("p t i -> p (t i)")
                for n, w in enumerate((w_gate, w_up)):
                    dst = XT[:, 3 * n:3 * n + 3, :]
                    sp.dma_start(dst[:, 0:2, :], w[0:2 * P, :].rearrange("(c p) k -> p c k", p=P)).then_inc(s_wload, 16)
                    sp.dma_start(dst[0:I - 2 * P, 2, :], w[2 * P:I, :]).then_inc(s_wload, 16)
                sp.dma_start(hsf[:, 0:I], w_down).then_inc(s_wload, 16)

            def iteration(it):
                for kind, a, i in of(it):
                    if kind == "XN":
                        if not zero(i):
                            sp.wait_ge(s_xused, i)
                        sp.dma_start(xin[:, :, :], x_v[i]).then_inc(s_x, 16)
                    if kind == "OS":
                        if not zero(i):
                            sp.wait_ge(s_yr, cnt(i, 2, 0))
                        sp.dma_start(xres[:, :, :], x_v[i]).then_inc(s_xres, 16)
                    if kind == "WO" and a == 5:
                        sp.wait_ge(s_yb, cnt(i, 1, 1))
                        sp.dma_start(out_v[i], yb[:, :, :]).then_inc(s_out, 16)
                    if kind == "LANES":
                        sp.wait_ge(read("GR", NH - 1), rv(i, "GR", NH - 1))
                        for q in range(NBL):
                            r = slice(BLK * q, BLK * q + BLK)
                            sp.dma_start(to_lanes[q].rearrange("u j i -> j u i"), UP[r, :, 0, r]).then_inc(s_diag, 16)
                        sp.wait_ge(s_diag, i * 16 * NBL + 16 * NBL)
                        sp.dma_start(laneA[:, :, :].rearrange("l j i -> l (j i)"),
                                     to_lanes.rearrange("q u j i -> (q u) (j i)")).then_inc(s_lin, 16)
                        sp.wait_ge(s_solved, cnt(i, 1, 1))
                        sp.dma_start(from_lanes.rearrange("q u j i -> (q u) (j i)"),
                                     laneX[:, :, :].rearrange("l j i -> l (j i)")).then_inc(s_lout, 16)
                        sp.wait_ge(s_lout, i * 16 + 16)
                        for q in range(NBL):
                            r = slice(BLK * q, BLK * q + BLK)
                            sp.dma_start(XT[r, :, r], from_lanes[q].rearrange("u j i -> j u i")).then_inc(s_xt, 16)

            run(sp, iteration)
            sp.wait_ge(s_out, 16 * NB)

        @block.gpsimd
        def _(pool):
            nc.gpsimd.memset(XT[:, :, :], 0.0).then_inc(s_setp, 1)
            nc.gpsimd.memset(ident[:, :], 0.0)
            nc.gpsimd.memset(ones[:, :], 1.0)
            nc.gpsimd.memset(negm[:, :, :], -30000.0)
            nc.gpsimd.memset(mhalf[:, :], -0.5)
            nc.gpsimd.memset(phalf[:, :], 0.5)
            nc.gpsimd.memset(id32[:, :, :], 0.0)
            nc.gpsimd.memset(pairsel[:, :], 1.0).then_inc(s_setp, 1)
            pool.wait_ge(s_setp, 2)
            nc.gpsimd.affine_select(out=ident[:, :], in_=ident[:, :], compare_op=ALU.not_equal, fill=1.0,
                                    base=0, pattern=[[-1, P]], channel_multiplier=1)
            nc.gpsimd.affine_select(out=mle[:, :], in_=ones[:, :], compare_op=ALU.is_ge, fill=0.0,
                                    base=0, pattern=[[1, P]], channel_multiplier=-1)
            nc.gpsimd.affine_select(out=mgt[:, :], in_=ones[:, :], compare_op=ALU.is_gt, fill=0.0,
                                    base=0, pattern=[[-1, P]], channel_multiplier=1)
            nc.gpsimd.affine_select(out=negm[:, :, :], in_=negm[:, :, :], compare_op=ALU.is_gt, fill=0.0,
                                    base=0, pattern=[[0, 4], [-1, P]], channel_multiplier=1)
            nc.gpsimd.affine_select(out=id32[:, :, :], in_=id32[:, :, :], compare_op=ALU.not_equal, fill=1.0,
                                    base=0, pattern=[[1, BLK], [-1, BLK]], channel_multiplier=0)
            nc.gpsimd.affine_select(out=pairsel[:, :], in_=pairsel[:, :], compare_op=ALU.is_ge, fill=0.0,
                                    base=0, pattern=[[-DK, 2]], channel_multiplier=1).then_inc(s_setp, 1)
            pool.wait_ge(s_setp, 3)
            nc.gpsimd.affine_select(out=pairsel[:, :], in_=pairsel[:, :], compare_op=ALU.is_gt, fill=0.0,
                                    base=DK, pattern=[[DK, 2]], channel_multiplier=-1)
            nc.gpsimd.tensor_copy(identb[:, :], ident[:, :]).then_inc(s_setp, 1)

            chain = [0, 0, 0]

            def iteration(it):
                first_it = isinstance(it, int) and it < 0
                i0, base = (0, 0) if first_it else (it, chain[2])
                if not first_it:
                    chain[1] = chain[0]

                def link(ins):
                    chain[1] += 1
                    ins.then_inc(s_pch, 1)
                    pool.wait_ge(s_pch, i0 * base + chain[1])

                for kind, a, i in of(it):
                    if kind == "XN":
                        pool.wait_ge(s_var, cnt(i, 1, 1))
                        nc.gpsimd.tensor_tensor(out=rstd[:, :], in0=veps[:, :], in1=mhalf[:, 0:NT],
                                                op=ALU.pow).then_inc(s_rstd, 1)
                    if kind == "DD":
                        n = dds.index(a)
                        if n == 0:
                            pool.wait_ge(s_g, cnt(i, 1, 1))
                        if n >= 2:
                            pool.wait_ge(full("DD", dds[n - 2]), rv(i, "DD", dds[n - 2]))
                        elif not zero(i):
                            pool.wait_ge(full("DD", dds[n + 4]), rv(i - 1, "DD", dds[n + 4]))
                        gf = g[:, :, :].rearrange("p t h -> p (t h)")[:, 4 * a:4 * a + 4]
                        nc.gpsimd.tensor_tensor(out=gm[:, n % 2, :, :], in0=bc(gf, 2, P),
                                                in1=bc(mle[:, :], 1, 4), op=ALU.mult).then_inc(s_gm, 1)
                    if kind == "CJ":
                        pool.wait_ge(read("SS", NP - 1), rv(i, "SS", NP - 1))
                        nc.gpsimd.tensor_tensor(out=sqk[:, :], in0=sse[:, 0, :, :].rearrange("p t h -> p (t h)"),
                                                in1=phalf[:, :], op=ALU.pow).then_inc(s_sqk, 1)
                    if kind == "LANES":
                        if not zero(i):
                            pool.wait_ge(s_lout, i * 16)
                            hold(pool)
                        link(nc.gpsimd.tensor_copy(laneX[:, :, :], id32[0:96, :, :]))
                        pool.wait_ge(s_lin, i * 16 + 16)
                        for j in range(BLK - 1):
                            n = BLK - 1 - j
                            t = laneT[:, 0:j + 1, 0:n]
                            link(nc.gpsimd.tensor_tensor(out=t, in0=laneX[:, 0:j + 1, j:j + 1].broadcast_to([96, j + 1, n]),
                                                         in1=laneA[:, j:j + 1, j + 1:BLK].broadcast_to([96, j + 1, n]),
                                                         op=ALU.mult))
                            w = laneX[:, 0:j + 1, j + 1:BLK]
                            ins = nc.gpsimd.tensor_tensor(out=w, in0=w, in1=t, op=ALU.subtract)
                            if j < BLK - 2:
                                link(ins)
                            else:
                                ins.then_inc(s_solved, 1)
                        for q in range(NBL):
                            r = slice(BLK * q, BLK * q + BLK)
                            hold(pool)
                            link(nc.gpsimd.memset(UP[r, :, 0, r], 0.0))
                        pool.sem_inc(s_zero, 1)
                    if kind == "OS":
                        pool.wait_ge(s_ov, cnt(i, 1, 1))
                        nc.gpsimd.tensor_tensor(out=rO[:, :], in0=ov[:, :], in1=mhalf[:, 0:NU],
                                                op=ALU.pow).then_inc(s_ro, 1)

            def counted(it):
                iteration(it)
                if isinstance(it, int) and it == -1:
                    chain[0] = chain[1]
                if isinstance(it, int) and it == 0:
                    chain[2] = chain[1] - chain[0]

            run(pool, counted)

        @block.scalar
        def _(act):
            act.wait_ge(s_wload, 16 * 19)
            nc.scalar.activation(negA[:, :], negA[:, :], ACT.Exp).then_inc(s_seta, 1)
            chain = [0, 0, 0]

            def iteration(it):
                first_it = isinstance(it, int) and it < 0
                i0, base = (0, 0) if first_it else (it, chain[2])
                if not first_it:
                    chain[1] = chain[0]

                def link(ins):
                    chain[1] += 1
                    ins.then_inc(s_ach, 1)
                    act.wait_ge(s_ach, i0 * base + chain[1])

                for kind, a, i in of(it):
                    b = bank(kind, a) if kind in RING else None
                    if kind in RING and kind not in ("ZB", "SS", "GR", "KT", "VT"):
                        act.wait_ge(full(kind, a), rv(i, kind, a))
                    if kind == "XN":
                        nc.scalar.activation(xnT[:, :], b[:, 0:T], ACT.Copy).then_inc(read("XN", 0), 1)
                    if kind == "ZB":
                        act.wait_ge(s_z, cnt(i, 1, 1))
                        nc.scalar.activation(eb[:, :, :], z[:, :, NH:], ACT.Exp, scale=-1.0)
                        link(nc.scalar.activation(ez[:, :, :], nabs[:, :, :], ACT.Exp))
                        nc.scalar.activation(lz[:, :, :], ez[:, :, :], ACT.Ln, bias=1.0).then_inc(s_ez, 1)
                    if kind == "GC":
                        nc.scalar.activation(eGR[:, :, :].rearrange("p a u -> p (a u)"), b[:, 0:2 * NU],
                                             ACT.Exp).then_inc(read("GC", 0), 1)
                    if kind == "DD":
                        nc.scalar.activation(UP[:, 4 * a:4 * a + 4, 1, :], b[:, :], ACT.Exp)\
                          .then_inc(read("DD", a), 1)
                    if kind == "QK":
                        KQ = kq(1)
                        for w in range(2):
                            ins = nc.scalar.activation(KQ[:, a, w, :], b[:, w * T:(w + 1) * T], ACT.Copy,
                                                       scale=ckq[:, w, a, TAPS - 1:TAPS])
                        ins.then_inc(s_tap, 1)
                    if kind == "SS":
                        KQ = kq(1)
                        act.wait_ge(read("QK", a), rv(i, "QK", a))
                        nc.scalar.activation(KQ[:, a, :, :], KQ[:, a, :, :], ACT.Silu).then_inc(s_kq, 1)
                        act.wait_ge(s_kq, cnt(i, NP, a + 1))
                        nc.scalar.activation(sq[:, a % 2, :, :], KQ[:, a, :, :], ACT.Square).then_inc(s_sq, 1)
                    if kind == "VP":
                        for n in range(2):
                            h = 2 * a + n
                            ins = nc.scalar.activation(vc[:, a % 2, n, :], b[:, n * T:(n + 1) * T], ACT.Copy,
                                                       scale=cvv[:, h, TAPS - 1:TAPS])
                        ins.then_inc(s_vtap, 1)
                    if kind == "VT":
                        act.wait_ge(read("VP", a), rv(i, "VP", a))
                        nc.scalar.activation(vc[:, a % 2, :, :], vc[:, a % 2, :, :], ACT.Silu).then_inc(s_vs, 1)
                    if kind == "GP":
                        t, q = a % 2, a // 2
                        nc.scalar.activation(Gt[:, t, 4 * q:4 * q + 4, :], b[:, :], ACT.Silu).then_inc(read(kind, a), 1)
                    if kind == "XQ":
                        nc.scalar.activation(xqT[:, :], b[:, 0:T], ACT.Copy).then_inc(read("XQ", 0), 1)
                    if kind == "FU":
                        nc.scalar.activation(hs[:, a, :], b[:, 0:I], ACT.Silu).then_inc(read("FU", a, 0), 1)
                    if kind == "HT":
                        for c in range(3):
                            m = min(P, I - c * P)
                            ins = nc.scalar.activation(hT[0:m, c, a, :], b[0:m, c * P:c * P + P], ACT.Copy)
                        ins.then_inc(read("HT", a), 1)
                    if kind == "SLOT":
                        h = stage(a, 0)
                        if h is not None:
                            act.wait_ge(s_wa, cnt(i, NH, h + 1))
                            nc.scalar.activation(Wm[:, h % 2, :, :, :].rearrange("p t w n -> p (t w n)"), BW[:, :],
                                                 ACT.Copy).then_inc(s_wr, 1)
                        if a in E_SLOTS:
                            act.wait_ge(s_be, cnt(i, len(E_SLOTS), E_SLOTS.index(a) + 1))
                            h = stage(a, 3)
                            if h is not None:
                                ins = nc.scalar.activation(eps0[:, h % 6, :], BE[:, 0:P], ACT.Copy)
                            h = stage(a, 4)
                            if h is not None:
                                ins = nc.scalar.activation(Sb[krows(h), h % 2, :], BE[krows(h), P:2 * P], ACT.Copy)
                            h = stage(a, 6)
                            if h is not None:
                                ins = nc.scalar.activation(eps1[:, h % 2, :], BE[:, 2 * P:3 * P], ACT.Copy)
                            ins.then_inc(s_er, 1)
                        h = stage(a, 8)
                        if h is not None:
                            out_squares(i, h, link)
                    if kind == "OS":
                        for h in range(NH + 7 - 8, NH):
                            out_squares(i, h, link)
                    if kind == "OT":
                        act.wait_ge(s_otf, cnt(i, 6, a + 1))
                        nc.scalar.activation(otb[:, a % 2, :, :], (BE, BO)[a % 2][:, :], ACT.Copy).then_inc(s_otr, 1)

            def out_squares(i, h, link):
                act.wait_ge(s_or, cnt(i, len(O_SLOTS), O_SLOTS.index(h + 7) + 1))
                for t in range(NT):
                    u = t * NH + h
                    link(nc.scalar.activation(junk[:, :], V[:, t, h, :], ACT.Square,
                                              accum_out=ssO[:, u:u + 1]))
                act.sem_inc(s_osum, 1)

            def counted(it):
                iteration(it)
                if isinstance(it, int) and it == -1:
                    chain[0] = chain[1]
                if isinstance(it, int) and it == 0:
                    chain[2] = chain[1] - chain[0]

            run(act, counted)

        @block.vector
        def _(dve):
            total = [0]

            def setup_link(ins):
                total[0] += 1
                ins.then_inc(s_dch, 1)
                dve.wait_ge(s_dch, total[0])

            def quantise(dst, src, n, link):
                nb = n // QB
                v, c, tt = qv[:, 0:n], qc[:, 0:n], qt[:, 0:n]
                by = lambda ap: ap.rearrange("p (b e) -> p b e", e=QB)
                link(nc.vector.tensor_reduce(qm[:, 0:nb], by(src), AX.X, ALU.max, apply_absolute_value=True))
                link(nc.vector.tensor_scalar(qs[:, 0:nb], qm[:, 0:nb], 1.0 / 6.0, 1e-12, ALU.mult, ALU.max))
                link(nc.vector.reciprocal(qr[:, 0:nb], qs[:, 0:nb]))
                link(nc.vector.tensor_tensor(by(v), by(src), bc(qr[:, 0:nb], 2, QB), ALU.mult))
                link(nc.vector.tensor_scalar(v.bitcast(U32), v.bitcast(U32), 0x7FFFFFFF, None, ALU.bitwise_and))
                link(nc.vector.tensor_scalar(c, v, 5.0, 2.0, ALU.is_gt, ALU.mult))
                link(nc.vector.scalar_tensor_tensor(c, v, 3.5, c, ALU.is_gt, ALU.add))
                link(nc.vector.scalar_tensor_tensor(c, v, 2.5, c, ALU.is_gt, ALU.add))
                link(nc.vector.tensor_scalar(tt, v, 1.75, None, ALU.is_gt))
                link(nc.vector.scalar_tensor_tensor(c, c, 2.0, tt, ALU.mult, ALU.add))
                for m in (1.25, 0.75, 0.25):
                    link(nc.vector.scalar_tensor_tensor(c, v, m, c, ALU.is_gt, ALU.add))
                link(nc.vector.scalar_tensor_tensor(v.bitcast(U32), src.bitcast(U32), 0x80000000, c.bitcast(U32),
                                                    ALU.bitwise_and, ALU.bitwise_or))
                link(nc.vector.tensor_scalar(qm[:, 0:nb], qs[:, 0:nb], 0.5, None, ALU.mult))
                return nc.vector.tensor_tensor(by(dst), by(v), bc(qm[:, 0:nb], 2, QB), ALU.mult)

            dve.wait_ge(s_wload, 16 * 19)
            dve.wait_ge(s_setp, 4)
            nc.vector.tensor_scalar(wo[:, :, :], wo[:, :, :], gw[:, 0:1], None, ALU.mult)
            for n in range(2):
                src = XT[:, 3 * n:3 * n + 3, :].rearrange("p c k -> p (c k)")
                setup_link(quantise(src, src, 3 * P, setup_link))
            dn = hs[:, :, :].rearrange("p t i -> p (t i)")[:, 0:I]
            setup_link(quantise(dn, dn, I, setup_link))
            dve.wait_ge(s_seta, 1)
            nc.vector.tensor_scalar(negA[:, :], negA[:, :], -1.0, None, ALU.mult).then_inc(s_setd, 1)
            dve.wait_ge(s_sett, 1)
            nc.vector.tensor_copy(wgu[:, 0, :], BW[:, 0:I])
            nc.vector.tensor_copy(wgu[:, 1, :], BF[:, 0:I])
            nc.vector.tensor_copy(wd[:, 0:2, :], BE[:, 0:2 * P])
            nc.vector.tensor_copy(wd[0:I - 2 * P, 2, :], BE[0:I - 2 * P, 2 * P:3 * P])
            setup_link(nc.vector.memset(XT[:, 0:6, :], 0.0))
            dve.sem_inc(s_setd, 1)
            chain = [0, total[0], 0]

            def iteration(it):
                first_it = isinstance(it, int) and it < 0
                i0, base = (0, 0) if first_it else (it, chain[2])
                if not first_it:
                    chain[1] = chain[0]

                def link(ins):
                    chain[1] += 1
                    ins.then_inc(s_dch, 1)
                    dve.wait_ge(s_dch, i0 * base + chain[1])

                def taps(acc, src, wt, last):
                    for s in range(1, TAPS):
                        for n in range(2):
                            ins = nc.vector.scalar_tensor_tensor(
                                acc[:, n, s:T], src[:, n * T:n * T + T - s], wt(n)[:, TAPS - 1 - s:TAPS - s],
                                acc[:, n, s:T], ALU.mult, ALU.add)
                        if s < TAPS - 1:
                            link(ins)
                    ins.then_inc(last, 1)

                for kind, a, i in of(it):
                    b = bank(kind, a) if kind in RING else None
                    if kind == "XN":
                        dve.wait_ge(s_x, i * 16 + 16)
                        for t in range(NT):
                            link(nc.vector.bn_stats(stats[:, t, :], xin[:, t, :]))
                            hold(dve)
                            link(nc.vector.bn_aggr(mv[:, t, :], stats[:, t, :]))
                        nc.vector.tensor_scalar(veps[:, :], mv[:, :, 1], 1e-5, None, ALU.add).then_inc(s_var, 1)
                        dve.wait_ge(s_rstd, cnt(i, 1, 1))
                        for t in range(NT):
                            ins = nc.vector.tensor_scalar(xn[:, t, :], xin[:, t, :], mv[:, t, 0:1], rstd[:, t:t + 1],
                                                          ALU.subtract, ALU.mult)
                        link(ins)
                        dve.sem_inc(s_xn, 1)
                        dve.sem_inc(s_xused, 1)
                    if kind == "ZB":
                        dve.wait_ge(full("ZB", 0), rv(i, "ZB", 0))
                        link(nc.vector.tensor_tensor(z[:, :, :], b[:, 0:4 * NH].rearrange("p (t n) -> p t n", t=NT),
                                                     bc(zbias[:, :], 1, NT), ALU.add))
                        dve.sem_inc(read("ZB", 0), 1)
                        link(nc.vector.tensor_scalar(nabs[:, :, :].bitcast(U32), z[:, :, 0:NH].bitcast(U32), 0x80000000, None,
                                                     ALU.bitwise_or))
                        dve.sem_inc(s_z, 1)
                        dve.wait_ge(s_ez, cnt(i, 1, 1))
                        link(nc.vector.scalar_tensor_tensor(sp[:, :, :], z[:, :, 0:NH], 0.0, lz[:, :, :],
                                                            ALU.max, ALU.add))
                        link(nc.vector.tensor_tensor(g[:, :, :], sp[:, :, :], bc(negA[:, :], 1, NT), ALU.mult))
                        dve.sem_inc(s_g, 1)
                        link(nc.vector.tensor_scalar(eb1[:, :, :], eb[:, :, :], 1.0, None, ALU.add))
                        link(nc.vector.reciprocal(beta[:, :, :], eb1[:, :, :]))
                    if kind == "CJ":
                        dve.wait_ge(read("SS", NP - 1), rv(i, "SS", NP - 1))
                        sk = sse[:, 0, :, :].rearrange("p t h -> p (t h)")
                        link(nc.vector.reciprocal(rinv[:, :], sk))
                        link(nc.vector.tensor_tensor(cj[:, :], rinv[:, :], beta[:, :, :].rearrange("p t h -> p (t h)"),
                                                     ALU.mult))
                        link(nc.vector.tensor_scalar(bq[:, :], sse[:, 1, :, :].rearrange("p t h -> p (t h)"),
                                                     1e-5 * DK, None, ALU.mult))
                        dve.wait_ge(read("GC", 0), rv(i, "GC", 0))
                        link(nc.vector.tensor_copy(eG[:, :], eGR[:, 0, :]))
                        link(nc.vector.tensor_scalar(negG[:, :], eGR[:, 0, :], -1.0, None, ALU.mult))
                        link(nc.vector.tensor_tensor(kr[:, :], cj[:, 0:NH], eGR[:, 1, 0:NH], ALU.mult))
                    if kind == "QK":
                        dve.wait_ge(s_tap, cnt(i, NP, a + 1))
                        taps(kq(1)[:, a, :, :], b, lambda n: ckq[:, n, a, :], read("QK", a))
                    if kind == "SS":
                        dve.wait_ge(full("SS", a), rv(i, "SS", a))
                        nc.vector.tensor_scalar(sse[:, :, :, 2 * a:2 * a + 2],
                                                b[:, 0:8].rearrange("p (w t n) -> p w t n", w=2, t=NT),
                                                1e-6, None, ALU.add).then_inc(read("SS", a), 1)
                    if kind == "VP":
                        dve.wait_ge(s_vtap, cnt(i, 6, a + 1))
                        taps(vc[:, a % 2, :, :], b, lambda n: cvv[:, 2 * a + n, :], read("VP", a))
                    if kind == "VT":
                        if a == 0:
                            dve.wait_ge(s_sqk, cnt(i, 1, 1))
                        dve.wait_ge(full("VT", a), rv(i, "VT", a))
                        for t in range(NT):
                            ins = nc.vector.tensor_tensor(V[:, t, 2 * a:2 * a + 2, :],
                                                          b[:, t * 2 * P:(t + 1) * 2 * P].rearrange("p (h n) -> p h n", h=2),
                                                          bc(sqk[:, t * NH + 2 * a:t * NH + 2 * a + 2], 2, P), ALU.mult)
                        ins.then_inc(read("VT", a), 1)
                    if kind == "GR":
                        dve.wait_ge(full("GR", a), rv(i, "GR", a))
                        if a == 0:
                            dve.wait_ge(read("DD", dds[-1]), rv(i, "DD", dds[-1]))
                        for t in range(NT):
                            u = t * NH + a
                            ins = nc.vector.scalar_tensor_tensor(
                                UP[:, u, :, :], b[:, t * 2 * P:(t + 1) * 2 * P].rearrange("p (k n) -> p k n", k=2),
                                cj[:, u:u + 1], bc(UP[:, u, 1, :], 1, 2), ALU.mult, ALU.mult)
                        ins.then_inc(read("GR", a), 1)
                    if kind == "KT":
                        dve.wait_ge(full("KT", a), rv(i, "KT", a))
                        h0 = NP * a
                        nc.vector.tensor_tensor(Kt[:, h0:h0 + NP, :],
                                                b[:, 0:NP * DK].rearrange("p (h d) -> p h d", d=DK),
                                                bc(kr[:, h0:h0 + NP], 2, DK), ALU.mult).then_inc(read("KT", a), 1)
                    if kind == "XQ":
                        xnf = xn[:, :, :].rearrange("p t d -> p (t d)")
                        link(quantise(xq[:, :, :].rearrange("p t d -> p (t d)"), xnf, NT * P, link))
                        dve.sem_inc(s_xqs, 1)
                    if kind == "FU":
                        dve.wait_ge(read("FU", a, 0), rv(i, "FU", a, 0))
                        dve.wait_ge(full("FU", a, 1), rv(i, "FU", a, 1))
                        nc.vector.tensor_tensor(hs[:, a, :], hs[:, a, :], bank("FU", a, 1)[:, 0:I], ALU.mult)\
                          .then_inc(read("FU", a, 1), 1)
                    if kind == "HQ":
                        hf = hs[:, :, :].rearrange("p t i -> p (t i)")
                        dve.wait_ge(read("FU", 1, 1), rv(i, "FU", 1, 1))
                        link(quantise(hf, hf, NQ, link))
                        dve.sem_inc(s_hq, 1)
                        dve.wait_ge(s_xt, i * 16 * NBL + 16 * NBL)
                        turn(i, 0)
                    if kind == "SLOT":
                        if 1 <= a + 1 < NH:
                            turn(i, a + 1)
                        if a in F_SLOTS:
                            dve.wait_ge(s_fb, cnt(i, len(F_SLOTS), F_SLOTS.index(a) + 1))
                            h = stage(a, 1)
                            if h is not None:
                                nc.vector.tensor_copy(W2[DK:P, h % 2, :, :], BF[DK:P, 2 * P:3 * P]
                                                      .rearrange("p (t n) -> p t n", t=NT))
                                ins = nc.vector.tensor_tensor(
                                    UP[:, h::NH, 0, :], XT[:, h::NH, :],
                                    BF[:, 0:2 * P].rearrange("p (t n) -> p t n", t=NT), ALU.subtract)
                            h = stage(a, 2)
                            if h is not None:
                                tu = UP[0:DK, h::NH, 0, DK:P]
                                ins = nc.vector.tensor_tensor(tu, tu, BF[0:DK, 3 * P:4 * P]
                                                              .rearrange("p (t n) -> p t n", t=NT), ALU.add)
                            ins.then_inc(s_fr, 1)
                        if a in O_SLOTS:
                            dve.wait_ge(s_bo, cnt(i, len(O_SLOTS), O_SLOTS.index(a) + 1))
                            h = stage(a, 5)
                            if h is not None:
                                u = NH + h
                                v1 = V[:, 1, h, :]
                                nc.vector.scalar_tensor_tensor(v1, BO[:, 0:P], negG[:, u:u + 1], v1, ALU.mult, ALU.add)\
                                  .then_inc(s_r1, 1)
                                link(nc.vector.tensor_scalar(qse[:, h % 4, :], BO[:, P:2 * P], eG[:, u:u + 1], None,
                                                             ALU.mult))
                            h = stage(a, 7)
                            if h is not None:
                                nc.vector.tensor_copy(V[:, 0, h, :], BO[:, 2 * P:3 * P])
                                link(nc.vector.tensor_tensor(V[:, 1, h, :], BO[:, 3 * P:4 * P], qse[:, h % 4, :],
                                                             ALU.add))
                            dve.sem_inc(s_or, 1)
                    if kind == "OS":
                        dve.wait_ge(s_osum, cnt(i, NH, NH))
                        link(nc.vector.scalar_tensor_tensor(ov[:, :], ssO[:, :], 1.0 / P, bq[:, :], ALU.mult, ALU.add))
                        dve.sem_inc(s_ov, 1)
                    if kind == "OG":
                        dve.wait_ge(s_ro, cnt(i, 1, 1))
                        for c in range(6):
                            t, q = c // 3, c % 3
                            dve.wait_ge(read("GP", t + 2 * q), rv(i, "GP", t + 2 * q))
                            for h in range(4 * q, 4 * q + 4):
                                u = t * NH + h
                                v = V[:, t, h, :]
                                ins = nc.vector.scalar_tensor_tensor(v, v, rO[:, u:u + 1], Gt[:, t, h, :],
                                                                     ALU.mult, ALU.mult)
                            ins.then_inc(s_og, 1)
                    if kind == "WO" and a % 3 == 2:
                        t = a // 3
                        dve.wait_ge(s_y, cnt(i, 2, t + 1))
                        if t == 0 and not zero(i):
                            dve.wait_ge(s_out, i * 16)
                        if t == 0:
                            dve.wait_ge(s_xres, i * 16 + 16)
                        ins = nc.vector.tensor_tensor(yb[:, t, :], (BW, BF)[t][:, 0:P], xres[:, t, :], ALU.add)
                        ins.then_inc(s_yr, 1)
                        if t == 1:
                            dve.wait_ge(s_yr, cnt(i, 2, 2))
                            dve.sem_inc(s_yb, 1)

            def turn(i, h):
                if h >= 2:
                    dve.wait_ge(s_wa, cnt(i, NH, h - 1))
                for t in range(NT):
                    ins = nc.vector.transpose(Xr[:, h % 2, t, :], XT[:, t * NH + h, :])
                ins.then_inc(s_xr, 1)

            def counted(it):
                iteration(it)
                if isinstance(it, int) and it == -1:
                    chain[0] = chain[1]
                if isinstance(it, int) and it == 0:
                    chain[2] = chain[1] - chain[0]

            run(dve, counted)

        @block.tensor
        def _(pe):
            mm = nc.tensor.matmul
            pe.wait_ge(s_setp, 4)
            pe.wait_ge(s_setd, 1)
            for n, b in enumerate((BW, BF)):
                for c in range(3):
                    m = min(P, I - c * P)
                    ins = nc.tensor.transpose(b[:, c * P:c * P + m], XT[0:m, 3 * n + c, :], ident[0:m, 0:m])
            dn = hs[:, :, :].rearrange("p t i -> p (t i)")
            for c in range(3):
                m = min(P, I - c * P)
                ins = nc.tensor.transpose(BE[0:m, c * P:c * P + P], dn[:, c * P:c * P + m], ident[:, :])
            ins.then_inc(s_sett, 1)
            pe.wait_ge(s_setd, 2)

            def iteration(it):
                def take(kind, a, j=0):
                    b, n = ring[kind, a, j]
                    if n or not zero(i):
                        pe.wait_ge(ring_read[b], i * ring_uses[b] + n)
                    return R[b]

                for kind, a, i in of(it):
                    if kind == "XN":
                        b = take("XN", 0)
                        pe.wait_ge(s_xn, cnt(i, 1, 1))
                        for t in range(NT):
                            ins = nc.tensor.transpose(b[:, t * P:t * P + P], xn[:, t, :], ident[:, :])
                        ins.then_inc(full("XN", 0), 1)
                    if kind == "ZB":
                        b = take("ZB", 0)
                        pe.wait_ge(read("XN", 0), rv(i, "XN", 0))
                        for t in range(NT):
                            o = t * P
                            ins = mm(b[:, t * 2 * NH:(t + 1) * 2 * NH], xnT[:, o:o + P], wzb[:, :], start=True, stop=True)
                        ins.then_inc(full("ZB", 0), 1)
                    if kind == "GC":
                        b = take("GC", 0)
                        pe.wait_ge(s_g, cnt(i, 1, 1))
                        gf = g[:, :, :].rearrange("p t h -> p (t h)")
                        mm(b[:, 0:NU], mle[:, :], gf, start=True, stop=True)
                        mm(b[:, NU:2 * NU], mgt[:, :], gf, start=True, stop=True).then_inc(full("GC", 0), 1)
                    if kind == "DD":
                        b = take("DD", a)
                        n = dds.index(a)
                        pe.wait_ge(s_gm, cnt(i, 6, n + 1))
                        mm(b[:, :], mgt[:, :], gm[:, n % 2, :, :].rearrange("p u n -> p (u n)"), start=True, stop=False)
                        mm(b[:, :], identb[:, :], negm[:, :, :].rearrange("p u n -> p (u n)"), start=False, stop=True)\
                            .then_inc(full("DD", a), 1)
                    if kind == "QK":
                        b = take("QK", a)
                        for w in range(2):
                            ins = mm(b[:, w * T:(w + 1) * T], wqk[:, w, a * P:(a + 1) * P], xnT[:, :],
                                     start=True, stop=True)
                        ins.then_inc(full("QK", a), 1)
                    if kind == "SS":
                        b = take("SS", a)
                        pe.wait_ge(s_sq, cnt(i, NP, a + 1))
                        for w in range(2):
                            for t in range(NT):
                                o = (w * NT + t) * 2
                                ins = mm(b[:, o:o + 2], sq[:, a % 2, w, t * P:(t + 1) * P], pairsel[:, :],
                                         start=True, stop=True)
                        ins.then_inc(full("SS", a), 1)
                    if kind == "GR":
                        b = take("GR", a)
                        r, p, KQ = krows(a), a // 2, kq(1)
                        for t in range(NT):
                            ts = slice(t * P, t * P + P)
                            ins = mm(b[:, t * 2 * P:(t + 1) * 2 * P], KQ[r, p, 0, ts], KQ[r, p, :, ts],
                                     start=True, stop=True)
                        ins.then_inc(full("GR", a), 1)
                    if kind == "KT":
                        b, KQ = take("KT", a), kq(1)
                        for n in range(3):
                            ins = nc.tensor.transpose(b[:, n * P:n * P + P], KQ[:, 3 * a + n, 0, 0:P], ident[:, :])
                        ins.then_inc(full("KT", a), 1)
                    if kind == "VP":
                        b = take("VP", a)
                        for n in range(2):
                            h = 2 * a + n
                            ins = mm(b[:, n * T:(n + 1) * T], wv[:, h * P:(h + 1) * P], xnT[:, :],
                                     start=True, stop=True)
                        ins.then_inc(full("VP", a), 1)
                    if kind == "VT":
                        b = take("VT", a)
                        pe.wait_ge(s_vs, cnt(i, 6, a + 1))
                        for t in range(NT):
                            for n in range(2):
                                o = (t * 2 + n) * P
                                ins = nc.tensor.transpose(b[:, o:o + P], vc[:, a % 2, n, t * P:(t + 1) * P], ident[:, :])
                        ins.then_inc(full("VT", a), 1)
                    if kind == "GP":
                        b = take("GP", a)
                        t, q = a % 2, a // 2
                        o = t * P
                        mm(b[:, :], xnT[:, o:o + P], wg[:, q * 512:(q + 1) * 512], start=True, stop=True)\
                            .then_inc(full("GP", a), 1)
                    if kind == "XQ":
                        b = take("XQ", 0)
                        pe.wait_ge(s_xqs, cnt(i, 1, 1))
                        for t in range(NT):
                            ins = nc.tensor.transpose(b[:, t * P:t * P + P], xq[:, t, :], ident[:, :])
                        ins.then_inc(full("XQ", 0), 1)
                    if kind == "FU":
                        pe.wait_ge(read("XQ", 0), rv(i, "XQ", 0))
                        for j in range(2):
                            b = take("FU", a, j)
                            mm(b[:, 0:I], xqT[:, a * P:(a + 1) * P], wgu[:, j, :], start=True, stop=True)\
                                .then_inc(full("FU", a, j), 1)
                    if kind == "HT":
                        b = take("HT", a)
                        pe.wait_ge(s_hq, cnt(i, 1, 1))
                        for c in range(3):
                            m = min(P, I - c * P)
                            ins = nc.tensor.transpose(b[0:m, c * P:c * P + P], hs[:, a, c * P:c * P + m], ident[:, :])
                        ins.then_inc(full("HT", a), 1)
                    if kind == "SLOT":
                        h = stage(a, 0)
                        if h is not None:
                            if h == 0:
                                pe.wait_ge(s_zero, cnt(i, 1, 1))
                                if not zero(i):
                                    pe.wait_ge(s_yr, cnt(i, 2, 0))
                            else:
                                pe.wait_ge(s_wr, cnt(i, NH, h))
                            pe.wait_ge(s_xr, cnt(i, NH, h + 1))
                            for t in range(NT):
                                u = t * NH + h
                                mm(BW[:, t * 2 * P:t * 2 * P + P], Xr[:, h % 2, t, :], UP[:, u, 0, :], start=True, stop=True)
                                ins = mm(BW[:, t * 2 * P + P:(t + 1) * 2 * P], UP[:, u, 0, :], Xr[:, h % 2, t, :],
                                         start=True, stop=True)
                            ins.then_inc(s_wa, 1)
                        if a in F_SLOTS:
                            n = F_SLOTS.index(a)
                            if n:
                                pe.wait_ge(s_fr, cnt(i, len(F_SLOTS), n))
                            h = stage(a, 1)
                            if h is not None:
                                pe.wait_ge(s_wr, cnt(i, NH, h + 1))
                                for t in range(NT):
                                    u = t * NH + h
                                    mm(BF[:, t * P:t * P + P], Wm[:, h % 2, t, 1, :], XT[:, u, :], start=True, stop=True)
                                    ins = mm(BF[DK:P, 2 * P + t * DK:2 * P + (t + 1) * DK], Wm[:, h % 2, t, 0, DK:P],
                                             Wm[:, h % 2, t, 1, 0:DK], start=True, stop=True)
                            h = stage(a, 2)
                            if h is not None:
                                hold(pe)
                                for t in range(NT):
                                    u = t * NH + h
                                    ins = mm(BF[0:DK, 3 * P + t * DK:3 * P + (t + 1) * DK], W2[DK:P, h % 2, t, :],
                                             UP[DK:P, u, 0, DK:P], start=True, stop=True)
                            ins.then_inc(s_fb, 1)
                        if a in E_SLOTS:
                            n = E_SLOTS.index(a)
                            if n:
                                pe.wait_ge(s_er, cnt(i, len(E_SLOTS), n))
                            h = stage(a, 3)
                            if h is not None:
                                if h == 0:
                                    pe.wait_ge(read("VT", 5), rv(i, "VT", 5))
                                pe.wait_ge(s_fr, cnt(i, len(F_SLOTS), F_SLOTS.index(h + 2) + 1))
                                ins = mm(BE[:, 0:P], UP[:, h, 0, :], V[:, 0, h, :], start=True, stop=True)
                            h = stage(a, 4)
                            if h is not None:
                                if h == 0:
                                    pe.wait_ge(read("KT", 0), rv(i, "KT", 0))
                                    pe.wait_ge(read("KT", 1), rv(i, "KT", 1))
                                ins = mm(BE[krows(h), P:2 * P], Kt[:, h, :], eps0[:, h % 6, :], start=True, stop=True)
                            h = stage(a, 6)
                            if h is not None:
                                pe.wait_ge(s_r1, cnt(i, NH, h + 1))
                                ins = mm(BE[:, 2 * P:3 * P], UP[:, NH + h, 0, :], V[:, 1, h, :], start=True, stop=True)
                            ins.then_inc(s_be, 1)
                        if a in O_SLOTS:
                            n = O_SLOTS.index(a)
                            if n:
                                pe.wait_ge(s_or, cnt(i, len(O_SLOTS), n))
                            h = stage(a, 5)
                            KQ = kq(0)
                            if h is not None:
                                for w in range(2):
                                    ins = mm(BO[:, w * P:(w + 1) * P], KQ[krows(h), h // 2, w, P:2 * P], Sb[krows(h), h % 2, :],
                                             start=True, stop=True)
                            h = stage(a, 7)
                            if h is not None:
                                if a not in E_SLOTS:
                                    pe.wait_ge(s_er, cnt(i, len(E_SLOTS), len(E_SLOTS)))
                                for t in range(NT):
                                    e = eps0[:, h % 6, :] if t == 0 else eps1[:, h % 2, :]
                                    ins = mm(BO[:, (2 + t) * P:(3 + t) * P], UP[:, t * NH + h, 1, :], e,
                                             start=True, stop=True)
                            ins.then_inc(s_bo, 1)
                    if kind == "OT":
                        b = (BE, BO)[a % 2]
                        t, q = a // 3, a % 3
                        if a >= 2:
                            pe.wait_ge(s_otr, cnt(i, 6, a - 1))
                        if a == 1:
                            pe.wait_ge(s_or, cnt(i, len(O_SLOTS), len(O_SLOTS)))
                        pe.wait_ge(s_og, cnt(i, 6, a + 1))
                        for n in range(4):
                            ins = nc.tensor.transpose(b[:, n * P:(n + 1) * P], V[:, t, 4 * q + n, :], ident[:, :])
                        ins.then_inc(s_otf, 1)
                    if kind == "WO":
                        t, q = a // 3, a % 3
                        y = (BW, BF)[t]
                        if q == 0:
                            if t == 0:
                                pe.wait_ge(read("HT", 0), rv(i, "HT", 0))
                                pe.wait_ge(read("HT", 1), rv(i, "HT", 1))
                            for c in range(3):
                                m = min(P, I - c * P)
                                mm(y[:, 0:P], hT[0:m, c, t, :], wd[0:m, c, :], start=(c == 0), stop=False)
                        pe.wait_ge(s_otr, cnt(i, 6, a + 1))
                        for n in range(4):
                            h = 4 * q + n
                            ins = mm(y[:, 0:P], otb[:, a % 2, n, :], wo[:, h, :], start=False, stop=(h == NH - 1))
                        if q == 2:
                            ins.then_inc(s_y, 1)

            run(pe, iteration)


_INS = ["L0_attn_hidden_states", "L0_attn_Wq", "L0_attn_Wk", "L0_attn_Wv", "L0_attn_Wg", "L0_attn_Wo",
        "L0_attn_conv_q", "L0_attn_conv_k", "L0_attn_conv_v", "L0_attn_Wgk", "L0_attn_Wb", "L0_attn_b_b",
        "L0_attn_A_log", "L0_attn_dt_bias", "L0_attn_g_norm_weight", "L0_ffn_w_gate", "L0_ffn_w_up",
        "L0_ffn_w_down"]


def kernel(**inputs):
    import numpy as _np
    import concourse.bacc as _bacc
    from concourse import mybir as _mybir
    from concourse.bass_utils import run_bass_kernel_spmd as _run

    nc = _bacc.Bacc("TRN2", target_bir_lowering=False, num_devices=1)
    arrays, args = {}, []
    for name in _INS:
        a = _np.ascontiguousarray(inputs[name])
        arrays[f"in_{name}_dram"] = a
        args.append(nc.dram_tensor(f"in_{name}_dram", a.shape, _mybir.dt.from_np(a.dtype), kind="ExternalInput").ap())
    shape = inputs["L0_attn_hidden_states"].shape
    o = nc.dram_tensor("out_0_dram", shape, _mybir.dt.from_np(_np.dtype("float32")), kind="ExternalOutput").ap()
    build(nc, *args, o, shape[0])
    r = _run(nc, [arrays], core_ids=[0])
    return r.results[0]["out_0_dram"]
```
